# Optimizing a Trainium2 kernel written in Bass

```python
import numpy as np
import jax
import jax.numpy as jnp

def _softmax(x, axis=-1):
    return jax.nn.softmax(x, axis=axis)

def _gelu(x):
    return jax.nn.gelu(x, approximate=True)

def _silu(x):
    return jax.nn.silu(x)

def _sigmoid(x):
    return jax.nn.sigmoid(x)

def _layernorm(x, axis=-1, eps=1e-05):
    m = jnp.mean(x, axis=axis, keepdims=True)
    v = jnp.var(x, axis=axis, keepdims=True)
    return (x - m) / jnp.sqrt(v + eps)

def _scatter_add(tgt, idx, src, axis=0):
    return tgt.at[idx].add(src)

def _segment_sum(src, seg, n):
    return jax.ops.segment_sum(src, seg, n)
kernel_name = 'mk_gnn_resnorm_d2_gnn_r8_b22fe6'

def setup_inputs(seed: int=0):
    np.random.seed(seed)
    _w = jnp.asarray

    def _rec_inputs():
        import jax
        import jax.numpy as jnp
        _gk = jax.random.key(seed)
        x = -0.0003713 + 1 * jax.random.normal(jax.random.fold_in(_gk, 1), (6250, 128), jnp.float32)
        src = jax.random.randint(jax.random.fold_in(_gk, 2), (200000,), 0, 6250, jnp.int32)
        dst = jnp.minimum((6250 * jax.random.uniform(jax.random.fold_in(_gk, 3), (200000,)) ** 2.0).astype(jnp.int32), 49999)
        _o = jnp.argsort(dst, stable=True)
        src = src[_o]
        dst = dst[_o]
        edge_attr_128 = -6.47781e-05 + 0.999943 * jax.random.normal(jax.random.fold_in(_gk, 12), (200000, 128), jnp.float32)
        return (x, src, dst, edge_attr_128)
    x, src, dst, edge_attr_128 = _rec_inputs()

    def _L0_gnn_setup():
        import jax, jax.numpy as jnp
        import numpy as np
        N_NODES = 12500
        N_EDGES = 200000
        N_NODE_F = 128
        N_EDGE_F = 128
        N_GLOBAL_F = 64
        N_GRAPHS = 256
        HIDDEN = 128
        IN_DIM = N_NODE_F + N_EDGE_F + N_GLOBAL_F
        key = jax.random.key(seed)
        k1, k2, k3, k4, k5, k6 = jax.random.split(key, 6)
        node_feats = jax.random.normal(k1, (N_NODES, N_NODE_F), dtype=jnp.float32)
        edge_feats = jax.random.normal(k2, (N_EDGES, N_EDGE_F), dtype=jnp.float32)
        global_feats = jax.random.normal(k3, (N_GRAPHS, N_GLOBAL_F), dtype=jnp.float32)
        W = jax.random.normal(k4, (HIDDEN, IN_DIM), dtype=jnp.float32) * (1.0 / np.sqrt(IN_DIM))
        edge_index = jax.random.randint(k5, (2, N_EDGES), 0, N_NODES, dtype=jnp.int64)
        batch = jnp.sort(jax.random.randint(k6, (N_NODES,), 0, N_GRAPHS, dtype=jnp.int64))
        return {'node_feats': node_feats, 'edge_feats': edge_feats, 'global_feats': global_feats, 'W': W, 'edge_index': edge_index, 'batch': batch}
    _L0_gnn_all = _L0_gnn_setup()
    _L0_gnn_in = {k: v for k, v in _L0_gnn_all.items() if k in ('global_feats', 'W')}
    del _L0_gnn_all

    def _L1_gnn_setup():
        import jax, jax.numpy as jnp
        import numpy as np
        LN_EPS = 1e-05
        N_NODES = 6250
        IN_DIM = 128
        OUT_DIM = 128
        N_EDGES = 100000

        def _ln(x, g, b):
            m = jnp.mean(x, axis=-1, keepdims=True)
            v = jnp.mean((x - m) ** 2, axis=-1, keepdims=True)
            return (x - m) * jax.lax.rsqrt(v + LN_EPS) * g + b
        key = jax.random.key(seed)
        ks = jax.random.split(key, 16)

        def lin(k, fan_in, fan_out):
            return jax.random.normal(k, (fan_in, fan_out), dtype=jnp.float32) / np.sqrt(fan_in)
        x = jax.random.normal(ks[0], (N_NODES, IN_DIM), dtype=jnp.float32)
        edge_index = jax.random.randint(ks[1], (2, N_EDGES), 0, N_NODES, dtype=jnp.int64)
        return {'x': x, 'edge_index': edge_index, 'W1': lin(ks[2], IN_DIM, OUT_DIM), 'b1': jnp.zeros((OUT_DIM,), jnp.float32), 'g1': jnp.ones((OUT_DIM,), jnp.float32), 'bt1': jnp.zeros((OUT_DIM,), jnp.float32), 'We1': lin(ks[3], 2 * OUT_DIM, OUT_DIM), 'be1': jnp.zeros((OUT_DIM,), jnp.float32), 'We2': lin(ks[4], OUT_DIM, 1), 'be2': jnp.zeros((1,), jnp.float32), 'Wn1': lin(ks[5], OUT_DIM, OUT_DIM), 'bn1': jnp.zeros((OUT_DIM,), jnp.float32), 'Wn2': lin(ks[6], OUT_DIM, 1), 'bn2': jnp.zeros((1,), jnp.float32), 'Wg': lin(ks[7], 2 * OUT_DIM, OUT_DIM), 'bg': jnp.zeros((OUT_DIM,), jnp.float32), 'g2': jnp.ones((OUT_DIM,), jnp.float32), 'bt2': jnp.zeros((OUT_DIM,), jnp.float32)}
    _L1_gnn_all = _L1_gnn_setup()
    _L1_gnn_in = {k: v for k, v in _L1_gnn_all.items() if k in ('W1', 'b1', 'g1', 'bt1', 'We1', 'be1', 'We2', 'be2', 'Wn1', 'bn1', 'Wn2', 'bn2', 'Wg', 'bg', 'g2', 'bt2')}
    del _L1_gnn_all
    return {'x': x, 'src': src, 'dst': dst, 'edge_attr_128': edge_attr_128, 'L0_gnn_global_feats': _L0_gnn_in['global_feats'], 'L0_gnn_W': _L0_gnn_in['W'], 'L1_gnn_W1': _L1_gnn_in['W1'], 'L1_gnn_b1': _L1_gnn_in['b1'], 'L1_gnn_g1': _L1_gnn_in['g1'], 'L1_gnn_bt1': _L1_gnn_in['bt1'], 'L1_gnn_We1': _L1_gnn_in['We1'], 'L1_gnn_be1': _L1_gnn_in['be1'], 'L1_gnn_We2': _L1_gnn_in['We2'], 'L1_gnn_be2': _L1_gnn_in['be2'], 'L1_gnn_Wn1': _L1_gnn_in['Wn1'], 'L1_gnn_bn1': _L1_gnn_in['bn1'], 'L1_gnn_Wn2': _L1_gnn_in['Wn2'], 'L1_gnn_bn2': _L1_gnn_in['bn2'], 'L1_gnn_Wg': _L1_gnn_in['Wg'], 'L1_gnn_bg': _L1_gnn_in['bg'], 'L1_gnn_g2': _L1_gnn_in['g2'], 'L1_gnn_bt2': _L1_gnn_in['bt2']}

def reference(x, src, dst, edge_attr_128, L0_gnn_global_feats, L0_gnn_W, L1_gnn_W1, L1_gnn_b1, L1_gnn_g1, L1_gnn_bt1, L1_gnn_We1, L1_gnn_be1, L1_gnn_We2, L1_gnn_be2, L1_gnn_Wn1, L1_gnn_bn1, L1_gnn_Wn2, L1_gnn_bn2, L1_gnn_Wg, L1_gnn_bg, L1_gnn_g2, L1_gnn_bt2):
    import jax
    import jax.numpy as jnp

    def _L0_gnn_ref(node_feats, edge_feats, global_feats, W, edge_index, batch):
        import jax, jax.numpy as jnp
        import numpy as np
        N_NODES = 12500
        N_EDGES = 200000
        N_NODE_F = 128
        N_EDGE_F = 128
        N_GLOBAL_F = 64
        N_GRAPHS = 256
        HIDDEN = 128
        IN_DIM = N_NODE_F + N_EDGE_F + N_GLOBAL_F
        n_nodes = node_feats.shape[0]
        idx_dst = edge_index[1]
        sums = jax.ops.segment_sum(edge_feats, idx_dst, num_segments=n_nodes)
        counts = jax.ops.segment_sum(jnp.ones((edge_feats.shape[0],), dtype=edge_feats.dtype), idx_dst, num_segments=n_nodes)
        mean_edge = sums / jnp.maximum(counts, 1.0)[:, None]
        out = jnp.concatenate([node_feats, mean_edge, global_feats[batch]], axis=1)
        h = jnp.einsum('ni,oi->no', out, W)
        return jax.nn.softplus(h) - jnp.log(jnp.asarray(2.0, dtype=h.dtype))

    def _L1_gnn_ref(x, edge_index, W1, b1, g1, bt1, We1, be1, We2, be2, Wn1, bn1, Wn2, bn2, Wg, bg, g2, bt2):
        import jax, jax.numpy as jnp
        import numpy as np
        LN_EPS = 1e-05
        N_NODES = 6250
        IN_DIM = 128
        OUT_DIM = 128
        N_EDGES = 100000

        def _ln(x, g, b):
            m = jnp.mean(x, axis=-1, keepdims=True)
            v = jnp.mean((x - m) ** 2, axis=-1, keepdims=True)
            return (x - m) * jax.lax.rsqrt(v + LN_EPS) * g + b
        n = x.shape[0]
        h = jax.nn.relu(_ln(x @ W1 + b1, g1, bt1))
        row, col = (edge_index[0], edge_index[1])
        h_src = h[row]
        ef = jnp.concatenate([h_src, h[col]], axis=1)
        edge_weights = jax.nn.sigmoid(jax.nn.relu(ef @ We1 + be1) @ We2 + be2)[:, 0]
        node_weights = jax.nn.sigmoid(jax.nn.relu(h @ Wn1 + bn1) @ Wn2 + bn2)[:, 0]
        _ = node_weights
        aggr = jax.ops.segment_sum(edge_weights[:, None] * h_src, col, num_segments=n)
        gate = jax.nn.sigmoid(jnp.concatenate([h, aggr], axis=-1) @ Wg + bg)
        h_new = gate * aggr + (1.0 - gate) * h
        return _ln(h_new, g2, bt2)
    edge_index = jnp.stack([src, dst])
    batch0 = jnp.zeros((6250,), jnp.int32)
    x = _layernorm(x + _L0_gnn_ref(x, edge_attr_128, L0_gnn_global_feats, L0_gnn_W, edge_index, batch0), axis=-1)
    x = _layernorm(x + _L1_gnn_ref(x, edge_index, L1_gnn_W1, L1_gnn_b1, L1_gnn_g1, L1_gnn_bt1, L1_gnn_We1, L1_gnn_be1, L1_gnn_We2, L1_gnn_be2, L1_gnn_Wn1, L1_gnn_bn1, L1_gnn_Wn2, L1_gnn_bn2, L1_gnn_Wg, L1_gnn_bg, L1_gnn_g2, L1_gnn_bt2), axis=-1)
    return x

_drawn_inputs = setup_inputs


def setup_inputs(seed=0):
    import zlib

    import numpy as np

    out = dict(_drawn_inputs(seed))
    spreads = {'L1_gnn_b1': (0.0, 0.1),
     'L1_gnn_g1': (1.0, 0.2),
     'L1_gnn_bt1': (0.0, 0.1),
     'L1_gnn_be1': (0.0, 0.479),
     'L1_gnn_bn1': (0.0, 0.1),
     'L1_gnn_bg': (0.0, 0.344),
     'L1_gnn_g2': (1.0, 0.2),
     'L1_gnn_bt2': (0.0, 0.1)}
    factors = {}
    for name, (base, spread) in spreads.items():
        noise = np.random.default_rng([zlib.crc32(name.encode()), seed]).standard_normal(out[name].shape)
        drawn = base * np.exp(spread * noise) if base else spread * noise
        out[name] = jnp.asarray(drawn.astype(out[name].dtype))
    for name, factor in factors.items():
        out[name] = (out[name] * factor).astype(out[name].dtype)
    return out
```

```python
from contextlib import ExitStack

import concourse.bass as bass
from concourse import mybir

F32 = mybir.dt.float32
BF16 = mybir.dt.bfloat16
I32 = mybir.dt.int32
ALU = mybir.AluOpType
ACT = mybir.ActivationFunctionType
AX = mybir.AxisListType
DVE = mybir.EngineType.DVE
SP = mybir.EngineType.SP

P = 128
J = 4
CHUNK = P * J
W = 40
PARTS = 3
WP = W * PARTS
REGS = 8
LN_EPS = 1e-5
LN2 = 0.6931471805599453
BANK = 512


def gnn_pair(nc, n_nodes, n_edges, io):
    n_chunks = -(-n_edges // CHUNK)
    last_start = n_edges - CHUNK
    repeated = (n_chunks * CHUNK - n_edges) // J
    n_blocks = -(-n_nodes // P)
    full_blocks = n_nodes // P
    tail_nodes = n_nodes - full_blocks * P
    padded = n_blocks * P
    columns = padded + W
    GB = 4
    n_groups = -(-n_blocks // GB)
    blocks_of = [min(GB, n_blocks - GB * g) for g in range(n_groups)]
    row_groups = -(-n_chunks // P)
    SUPER = 4
    n_supers = -(-n_chunks // SUPER)
    V_SLOTS, G_SLOTS, Q_SLOTS = 4, 6, 4

    ctx = ExitStack()
    with ctx:
        def sb(name, shape, dt=F32):
            return ctx.enter_context(nc.sbuf_tensor(name, shape, dt))

        def sem(name):
            return ctx.enter_context(nc.semaphore(name))

        src_table = nc.dram_tensor("src_table", (padded, 2 * P), F32).ap()
        dst_table = nc.dram_tensor("dst_table", (columns * PARTS, P), BF16).ap()

        sums = sb("sums", [P, 2, columns])
        aggr = sums[:, 0, :]
        x_rows = sb("x_rows", [P, n_blocks, P])
        gathered = x_rows[:, :, :].rearrange("p b f -> p (b f)")[:, 0:G_SLOTS * J * 2 * P] \
            .rearrange("p (s j f) -> p s j f", s=G_SLOTS, j=J)
        x1_rows = sb("x1_rows", [P, n_blocks, P])
        h_cols = sb("h_cols", [P, padded])
        ring = sb("ring", [P, 19 * BANK])
        edge_ring = ring[:, 0:V_SLOTS * SUPER * J * P].rearrange("p (s c j f) -> p s c j f", s=V_SLOTS, c=SUPER, j=J)
        x1_flat = x1_rows[:, :, :].rearrange("p b f -> p (b f)")
        lane_dst_i = x1_flat[:, 0:n_chunks * J].bitcast(I32).rearrange("p (c j) -> p c j", j=J)
        reach = x1_flat[0:1, n_chunks * J:n_chunks * J + n_chunks]
        chunk_rows = sb("chunk_rows", [P, n_chunks], I32)
        start_row = chunk_rows[0:1, :]
        start3_row = chunk_rows[32:33, :]
        end_row = chunk_rows[64:65, :]
        edge_row = sb("edge_row", [1, n_chunks], I32)
        lane_src = sb("lane_src", [P, n_chunks * J], I32)
        lane_dst = sb("lane_dst", [P, n_chunks, J])
        chunk_dst = ring[:, 0:row_groups * CHUNK].bitcast(I32).rearrange("p (g e) -> p g e", g=row_groups)
        extent = sb("extent", [P, row_groups, 2])
        diag = sb("diag", [P, 2, P])
        starts = sb("starts", [P, row_groups * P])
        widest = sb("widest", [1, 2])
        widest_i = sb("widest_i", [1, 1], I32)
        ident = sb("ident", [P, P])
        ident_b = sb("ident_b", [P, P], BF16)
        ones = sb("ones", [P, P])
        ones_b = sb("ones_b", [P, P], BF16)
        iota_i = sb("iota_i", [P, WP], I32)
        iota3 = sb("iota3", [P, WP])
        iota1_i = sb("iota1_i", [P, W], I32)
        iota1 = sb("iota1", [P, W])
        eps = sb("eps", [P, 1])
        w_node = sb("w_node", [P, P])
        w_edge = sb("w_edge", [P, P])
        w_glob = sb("w_glob", [64, P])
        glob_col = sb("glob_col", [64, 1])
        glob = sb("glob", [64, P])
        w1 = sb("w1", [P, P])
        we1_src = sb("we1_src", [P, P])
        we1_dst = sb("we1_dst", [P, P])
        wg_h = sb("wg_h", [P, P])
        wg_a = sb("wg_a", [P, P])
        bg_col = sb("bg_col", [P, 1])
        be2_all = sb("be2_all", [P, 1])
        rows = {n: sb(n + "_row", [1, P]) for n in ("b1", "be1")}
        wide = {n: sb(n + "_all", [P, P]) for n in ("g1", "bt1", "we2", "g2", "bt2")}
        onehot = sb("onehot", [P, 4, J, W])
        onehot3 = sb("onehot3", [P, 3, J, WP], BF16)
        onehot3_t = sb("onehot3_t", [WP, 2, J, P], BF16)
        window = sb("window", [WP, Q_SLOTS, P], BF16)
        logit = sb("logit", [P, 4, J])
        weight = sb("weight", [P, 4, J])
        weighted = sb("weighted", [P, 3, J, W])
        pad_rows = sb("pad_rows", [WP, P], BF16)
        shift = sb("shift", [P, 1])
        far_dst = sb("far_dst", [P, J])
        far_src = sb("far_src", [P, J], I32)
        far_token = sb("far_token", [P, J], I32)
        stats = sb("stats", [P, 2, GB, 6])
        moments = sb("moments", [P, 2, GB, 2])
        rstd = sb("rstd", [P, 2, GB])
        stats2 = sb("stats2", [P, 2, GB, 6])
        moments2 = sb("moments2", [P, 2, GB, 2])
        rstd2 = sb("rstd2", [P, 2, GB])

        at = [0]

        def temp(cols, dt=F32, depth=2):
            a = ring[:, at[0]:at[0] + cols * depth]
            at[0] += cols * depth
            a = a if dt == F32 else a.bitcast(dt)
            return a.rearrange("p (s c) -> p s c", s=depth)

        GC = GB * P
        pre = temp(GC)
        soft = temp(GC)
        y1 = temp(GC)
        x1_cols = temp(GC)
        z1 = temp(GC)
        rest = temp(GC)
        src_out = temp(2 * GC)
        dst_out = temp(GC * PARTS // 2, BF16)

        bank = [ctx.enter_context(nc.psum_tensor(f"bank{i}", [P, BANK], F32)) for i in range(8)]
        const_bank = bank[7]
        iota3_p = const_bank[:, 0:WP]
        iota1_p = const_bank[:, 128:128 + W]

        names = {}

        def done(name):
            if name not in names:
                names[name] = sem("s_" + name)
            return names[name]

        def need(eng, name, n):
            if n >= 0:
                eng.wait_ge(done(name), n + 1)

        def loaded(eng, name, n=1):
            eng.wait_ge(done(name), 16 * n)

        def slot_uses(k):
            return (n_groups - k + 1) // 2

        def whole_blocks(g):
            return blocks_of[g] - (1 if g == n_groups - 1 and tail_nodes else 0)

        def out_dmas(k, end):
            return sum((whole_blocks(g) > 0) + (whole_blocks(g) < blocks_of[g]) for g in range(k, end, 2))

        def block_cols(g):
            return slice(g * GC, g * GC + blocks_of[g] * P)

        def chunk_start(c):
            return min(c * CHUNK, last_start)

        edge_rows = io["edge_attr_128"]

        def edges_of(c, n):
            s = chunk_start(c)
            return edge_rows[s:s + n * CHUNK, :].rearrange("(c p j) f -> p c (j f)", c=n, j=J)

        def super_loads(s):
            first, end = s * SUPER, min((s + 1) * SUPER, n_chunks)
            if end < n_chunks:
                return [(first, end - first)]
            return ([(first, end - 1 - first)] if end - 1 > first else []) + [(end - 1, 1)]

        slot_total = [0] * V_SLOTS
        super_ready = []
        for s in range(n_supers):
            slot_total[s % V_SLOTS] += 16 * len(super_loads(s))
            super_ready.append(slot_total[s % V_SLOTS])
        edge_in = [sem(f"s_edge_in{i}") for i in range(V_SLOTS)]
        gather_in = [sem(f"s_gather_in{i}") for i in range(G_SLOTS)]
        window_in = [sem(f"s_window_in{i}") for i in range(Q_SLOTS)]
        XW_EVERY = 8

        def edge_sums(eng, out, values, hot):
            for j in range(J):
                eng.matmul(out[:, 0, :], values[:, j, :], hot[:, j, :], start=(j == 0), stop=(j == J - 1))
            half = hot.bitcast(BF16).rearrange("p j (w t) -> p j w t", t=2)
            for j in range(J):
                last = eng.matmul(out[:, 1, :], ones_b[:, :], half[:, j, :, 1], start=(j == 0), stop=(j == J - 1))
            return last

        def make_onehot(eng, out, dst):
            return eng.tensor_tensor(out, iota1[:, :].unsqueeze(1).to_broadcast([P, J, W]),
                                     dst.unsqueeze(2).to_broadcast([P, J, W]), ALU.is_equal)

        def make_onehot3(eng, out, dst):
            return eng.tensor_tensor(out, iota3_p.unsqueeze(1).to_broadcast([P, J, WP]),
                                     dst.unsqueeze(2).to_broadcast([P, J, WP]), ALU.is_equal)

        def turn_onehot3(eng, out, hot):
            for j in range(J):
                last = eng.transpose(out[:, j, :], hot[:, j, :], ident_b[:, :])
            return last

        def dst_part(eng, out, hot_t, win):
            for j in range(J):
                last = eng.matmul(out[:, j, :], hot_t[:, j, :], win, start=True, stop=True, skip_group_check=True)
            return last

        def add_src_part(eng, out, rows_):
            return eng.tensor_tensor(out, out, rows_[:, :, 0:P], ALU.add)

        def edge_dots(eng, out, hid):
            for j in range(J):
                last = eng.scalar_tensor_tensor(hid[:, j, :], hid[:, j, :], 0.0, wide["we2"][:, :], ALU.max,
                                                ALU.mult, accum_out=out[:, j:j + 1])
            return last

        def weigh(eng, out, dst, wt):
            for j in range(J):
                last = eng.tensor_scalar(out[:, j, :], iota1_p, dst[:, j:j + 1], wt[:, j:j + 1], ALU.is_equal, ALU.mult)
            return last

        def weighted_sums(eng, out, rows_, hot):
            for j in range(J):
                last = eng.matmul(out, rows_[:, j, P:2 * P], hot[:, j, :], start=(j == 0), stop=(j == J - 1))
            return last

        def add_window(eng, table, start, part):
            return eng.tensor_tensor(table[..., bass.ds(start, W)], table[..., bass.ds(start, W)], part, ALU.add)

        def load_starts(table, c, engine):
            n = min(REGS, n_chunks - c)
            top = n_nodes - 1 if table is not start3_row else PARTS * (n_nodes - 1)
            _, regs = nc.values_load_multi_w_load_instructions(
                table[0:1, c:c + n], engines=[engine], min_val=0, max_val=top,
                skip_runtime_bounds_check_because="destinations are node numbers")
            return regs

        def further_windows(eng, layer, body):
            need(eng, "widest", 0)
            reach_all = eng.value_load(widest_i[0:1, 0:1], min_val=0, max_val=n_nodes - 1)
            with eng.If(reach_all > W - 1):
                count = eng.alloc_register(f"item{layer}")
                eng.reg_mov(count, 0)
                with eng.Fori(0, n_chunks) as c:
                    first = eng.value_load(start_row[0:1, bass.ds(c, 1)], min_val=0, max_val=n_nodes - 1)
                    end = eng.value_load(end_row[0:1, bass.ds(c, 1)], min_val=0, max_val=n_nodes)
                    with eng.If(first + W < end):
                        with eng.Fori(first + W, end, W) as start:
                            eng.reg_add(count, count, 1)
                            body(eng.snap(count, min_val=1, max_val=1 << 20), c, start,
                                 first)

        def w1_bank(g):
            return bank[2 + 4 * (g % 2)]

        def turned(c):
            return bank[c % 2][0:WP, 0:J * P // 2].bitcast(BF16).rearrange("w (j e) -> w j e", j=J)

        def hidden(c):
            return bank[2 + c % 2][:, :].rearrange("p (j f) -> p j f", j=J)

        def window_out(c):
            return bank[4 + c % 2][:, 0:W]

        def edge_out(c):
            return bank[c % 4][:, 0:2 * W].rearrange("p (t w) -> p t w", t=2)

        block = ctx.enter_context(nc.Block())

        @block.sync
        def _(eng):
            for g in range(row_groups):
                n = min(P, n_chunks - g * P)
                eng.dma_start(chunk_dst[0:n, g, :], io["dst_by_chunk"][g * P:g * P + n, :]).then_inc(done("chunk_dst"), 16)
            eng.dma_start(lane_dst_i[:, :, :], io["dst_by_lane"]).then_inc(done("lane_dst_i"), 16)
            need(eng, "extent", 0)
            for s in range(n_supers):
                if s >= V_SLOTS:
                    need(eng, "edge_mm", (s - V_SLOTS + 1) * SUPER - 1)
                for c, n in super_loads(s):
                    k = c - s * SUPER
                    eng.dma_start(edge_ring[:, s % V_SLOTS, k:k + n, :, :].rearrange("p c j f -> p c (j f)"),
                                  edges_of(c, n)).then_inc(edge_in[s % V_SLOTS], 16)

            def far_edges(item, c, start, first):
                row = eng.value_load(edge_row[0:1, bass.ds(c, 1)], min_val=0, max_val=last_start // J)
                eng.wait_ge(done("far_acc"), item)
                eng.dma_start(edge_ring[:, 0, 0, :, :].rearrange("p j f -> p (j f)"),
                              edge_rows.rearrange("(r j) f -> r (j f)", j=J)[bass.ds(row, P), :]).then_inc(done("far_edges"), 16)

            need(eng, "edge_mm", n_chunks - 1)
            need(eng, "edge_row", 0)
            further_windows(eng, 0, far_edges)

            for g in range(n_groups):
                nb = blocks_of[g]
                need(eng, "src_rows", g)
                need(eng, "relu", g)
                eng.dma_start(src_table[g * GC:g * GC + nb * P, :].rearrange("(b p) f -> p b f", p=P),
                              src_out[:, g % 2, 0:nb * 2 * P].rearrange("p (b f) -> p b f", b=nb)).then_inc(done(f"src_table{g % 2}"), 16)
                need(eng, "part2", g)
                eng.dma_start(dst_table[g * GC * PARTS:(g * GC + nb * P) * PARTS, :].rearrange("(b p s) f -> p b (s f)", p=P, s=PARTS),
                              dst_out[:, g % 2, 0:nb * PARTS * P].rearrange("p (b f) -> p b f", b=nb)).then_inc(done(f"dst_table{g % 2}"), 16)
            need(eng, "pad_rows", 0)
            eng.dma_start(dst_table[padded * PARTS:columns * PARTS, :], pad_rows[:, :]).then_inc(done("dst_table_pad"), 16)
            loaded(eng, "dst_table_pad")
            for k in range(2):
                loaded(eng, f"dst_table{k}", slot_uses(k))
            for c in range(n_chunks):
                if c % REGS == 0:
                    regs = load_starts(start3_row, c, SP)
                need(eng, "hidden", c - Q_SLOTS)
                eng.dma_start(window[:, c % Q_SLOTS, :], dst_table[bass.ds(regs[c % REGS], WP), :]).then_inc(window_in[c % Q_SLOTS], 16)

            def far_window(item, c, start, first):
                row = eng.snap(start * PARTS, min_val=0, max_val=PARTS * n_nodes)
                eng.wait_ge(done("far_acc2"), item)
                eng.dma_start(window[:, 0, :], dst_table[bass.ds(row, WP), :]).then_inc(done("far_window"), 16)

            need(eng, "hidden", n_chunks - 1)
            further_windows(eng, 1, far_window)

            for g in range(n_groups):
                nb = blocks_of[g]
                need(eng, "out_rows", g)
                full = whole_blocks(g)
                tile = y1[:, g % 2, 0:nb * P].rearrange("p (b f) -> p b f", b=nb)
                if full:
                    eng.dma_start(io["out"][g * GC:g * GC + full * P, :].rearrange("(b p) f -> p b f", p=P),
                                  tile[:, 0:full, :]).then_inc(done(f"out{g % 2}"), 16)
                if full < nb:
                    eng.dma_start(io["out"][full_blocks * P:n_nodes, :], tile[0:tail_nodes, full, :]).then_inc(done(f"out{g % 2}"), 16)
            for k in range(2):
                loaded(eng, f"out{k}", out_dmas(k, n_groups))

        @block.gpsimd
        def _(eng):
            eng.memset(ident[:, :], 0.0).then_inc(done("blank"), 1)
            eng.memset(ident_b[:, :], 0.0).then_inc(done("blank"), 1)
            eng.memset(ones[:, :], 1.0)
            eng.memset(ones_b[:, :], 1.0)
            eng.memset(eps[:, :], LN_EPS)
            eng.memset(shift[:, :], 0.0)
            eng.iota(iota_i[:, :], pattern=[[1, W], [0, PARTS]], base=0, channel_multiplier=0)
            eng.iota(iota1_i[:, :], pattern=[[1, W]], base=0, channel_multiplier=0)
            eng.iota(edge_row[:, :], pattern=[[P, n_chunks]], base=0, channel_multiplier=0).then_inc(done("blank"), 1)
            need(eng, "blank", 2)
            for m in (ident, ident_b):
                last = eng.affine_select(out=m[:, :], in_=m[:, :], compare_op=ALU.not_equal, fill=1.0, base=0,
                                         pattern=[[-1, P]], channel_multiplier=1)
            last.then_inc(done("constants"), 1)
            eng.tensor_scalar(edge_row[:, :], edge_row[:, :], float(last_start // J), None, ALU.min).then_inc(done("edge_row"), 1)
            eng.memset(pad_rows[:, :], 0.0).then_inc(done("pad_rows"), 1)
            if tail_nodes:
                eng.memset(x_rows[:, full_blocks, :], 0.0)
                eng.memset(h_cols[:, n_nodes:padded], 0.0)
            eng.memset(sums[:, 0, :], 0.0)
            eng.memset(sums[:, 1, :], 0.0).then_inc(done("zeroed"), 1)

            def at_least_one(g):
                if g == 0:
                    need(eng, "acc_all", 0)
                cols = block_cols(g)
                eng.tensor_scalar(sums[:, 1, cols], sums[:, 1, cols], 1.0, None, ALU.max).then_inc(done("count"), 1)

            def mean(g):
                need(eng, "recip", g)
                cols = block_cols(g)
                eng.tensor_tensor(sums[:, 0, cols], sums[:, 0, cols], sums[:, 1, cols], ALU.mult).then_inc(done("mean"), 1)

            def gain(g):
                nb = blocks_of[g]
                need(eng, "norm2", g)
                z = z1[:, g % 2, 0:nb * P].rearrange("p (b f) -> p b f", b=nb)
                eng.tensor_tensor(z, z, wide["g1"][:, :].unsqueeze(1).to_broadcast([P, nb, P]), ALU.mult).then_inc(done("gain"), 1)
                need(eng, "gain", g)
                eng.tensor_tensor(z, z, wide["bt1"][:, :].unsqueeze(1).to_broadcast([P, nb, P]), ALU.add).then_inc(done("offset"), 1)

            loaded(eng, "small", N_SMALL)
            run_stages(n_groups, [(0, at_least_one), (0, mean), (NORM2_AT, gain)])

            loaded(eng, "lane_src")
            for k in range(2):
                loaded(eng, f"src_table{k}", slot_uses(k))
            need(eng, "res", n_groups - 1)
            for c in range(n_chunks):
                need(eng, "wsum", c - G_SLOTS)
                for j in range(J):
                    t = c * J + j
                    eng.indirect_dma_start(gathered[:, c % G_SLOTS, j, :], None, src_table,
                                           bass.IndirectOffsetOnAxis(ap=lane_src[:, t:t + 1], axis=0)).then_inc(gather_in[c % G_SLOTS], 16)

            def far_gather(item, c, start, first):
                eng.wait_ge(done("far_src"), item)
                eng.tensor_tensor(far_token[:, :], far_src[:, :], far_src[:, :], ALU.add).then_inc(done("far_token"), 1)
                for j in range(J):
                    eng.indirect_dma_start(gathered[:, 0, j, :], None, src_table,
                                           bass.IndirectOffsetOnAxis(ap=far_src[:, j:j + 1], axis=0)).then_inc(done("far_gather"), 16)

            need(eng, "wsum", n_chunks - 1)
            further_windows(eng, 1, far_gather)

            def gain2(g):
                nb = blocks_of[g]
                z = z1[:, g % 2, 0:nb * P].rearrange("p (b f) -> p b f", b=nb)
                need(eng, "out_norm", g)
                eng.tensor_tensor(z, z, wide["g2"][:, :].unsqueeze(1).to_broadcast([P, nb, P]), ALU.mult).then_inc(done("gain2"), 1)
                need(eng, "gain2", g)
                eng.tensor_tensor(z, z, wide["bt2"][:, :].unsqueeze(1).to_broadcast([P, nb, P]), ALU.add).then_inc(done("offset2"), 1)

            run_stages(n_groups, [(0, gain2)])

        @block.scalar
        def _(eng):
            def load(dst, src):
                eng.dma_start(dst, src).then_inc(done("small"), 16)

            small = [
                (w_node[:, :], io["L0_W_t"][0:P, :]), (w_edge[:, :], io["L0_W_t"][P:2 * P, :]),
                (w_glob[:, :], io["L0_W_t"][2 * P:2 * P + 64, :]),
                (glob_col[:, :], io["L0_gnn_global_feats"][0:1, :].rearrange("a k -> k a")),
                (w1[:, :], io["L1_gnn_W1"]), (we1_src[:, :], io["L1_gnn_We1"][0:P, :]),
                (we1_dst[:, :], io["L1_gnn_We1"][P:2 * P, :]), (wg_h[:, :], io["L1_gnn_Wg"][0:P, :]),
                (wg_a[:, :], io["L1_gnn_Wg"][P:2 * P, :]),
                (bg_col[:, :], io["L1_gnn_bg"].rearrange("(k a) -> k a", a=1)),
                (be2_all[:, :], io["L1_gnn_be2"].rearrange("(a k) -> a k", a=1).partition_broadcast(P)),
                (rows["b1"][:, :], io["L1_gnn_b1"].rearrange("(a k) -> a k", a=1)),
                (rows["be1"][:, :], io["L1_gnn_be1"].rearrange("(a k) -> a k", a=1)),
                (wide["g1"][:, :], io["L1_gnn_g1"].rearrange("(a k) -> a k", a=1).partition_broadcast(P)),
                (wide["bt1"][:, :], io["L1_gnn_bt1"].rearrange("(a k) -> a k", a=1).partition_broadcast(P)),
                (wide["we2"][:, :], io["L1_gnn_We2"].rearrange("k a -> a k").partition_broadcast(P)),
                (wide["g2"][:, :], io["L1_gnn_g2"].rearrange("(a k) -> a k", a=1).partition_broadcast(P)),
                (wide["bt2"][:, :], io["L1_gnn_bt2"].rearrange("(a k) -> a k", a=1).partition_broadcast(P)),
            ]
            assert len(small) == N_SMALL
            for dst, src in small:
                load(dst, src)
            need(eng, "zeroed", 0)
            eng.dma_start(h_cols[:, 0:n_nodes], io["x_t"]).then_inc(done("x_cols"), 16)
            eng.dma_start(x_rows[:, 0:full_blocks, :], io["x"][0:full_blocks * P, :].rearrange("(b p) f -> p b f", p=P)).then_inc(done("x_rows"), 16)
            if tail_nodes:
                eng.dma_start(x_rows[0:tail_nodes, full_blocks, :], io["x"][full_blocks * P:n_nodes, :]).then_inc(done("x_rows"), 16)
            eng.dma_start(lane_src[:, :], io["src_by_lane"]).then_inc(done("lane_src"), 16)

            eng.preload_act_table_set("natural_log_exp_and_others")
            for g in range(n_groups):
                nb = blocks_of[g]
                need(eng, "xw_mm", g)
                eng.activation(x1_rows[:, g * GB:g * GB + nb, :].rearrange("p b f -> p (b f)"),
                               bank[4 + g % 2][:, 0:nb * P], ACT.Copy).then_inc(done("xw"), 1)

            def softplus(g):
                n = blocks_of[g] * P
                t = soft[:, g % 2, 0:n]
                need(eng, "pre", g)
                need(eng, "soft_sum", g - 2)
                eng.activation(t, pre[:, g % 2, 0:n], ACT.Abs).then_inc(done("act"), 1)
                eng.wait_ge(done("act"), 2 * g + 1)
                eng.activation(t, t, ACT.Exp, scale=-1.0).then_inc(done("act"), 1)
                eng.wait_ge(done("act"), 2 * g + 2)
                eng.activation(t, t, ACT.Ln, bias=1.0).then_inc(done("softlog"), 1)

            def inverse_std(g, ready, out, mom, name, freed):
                nb = blocks_of[g]
                need(eng, ready, g)
                need(eng, freed, g - 2)
                o = out[:, g % 2, 0:nb]
                eng.activation(o, mom[:, g % 2, 0:nb, 1], ACT.Ln, bias=eps[:, 0:1]).then_inc(done(name + "_ln"), 1)
                need(eng, name + "_ln", g)
                eng.activation(o, o, ACT.Exp, scale=-0.5).then_inc(done(name), 1)

            def x1_turned(g):
                n = blocks_of[g] * P
                need(eng, "x1_turn", g)
                need(eng, "w1_mm", g - 2)
                eng.activation(x1_cols[:, g % 2, 0:n], bank[1][:, 0:n], ACT.Copy).then_inc(done("x1_cols"), 1)

            def relu(g):
                nb = blocks_of[g]
                need(eng, "offset", g)
                if g >= 2:
                    loaded(eng, f"src_table{g % 2}", g // 2)
                o = src_out[:, g % 2, 0:nb * 2 * P].rearrange("p (b f) -> p b f", b=nb)[:, :, P:2 * P]
                eng.activation(o, z1[:, g % 2, 0:nb * P].rearrange("p (b f) -> p b f", b=nb), ACT.Relu).then_inc(done("relu"), 1)

            def h_turned(g):
                n = blocks_of[g] * P
                need(eng, "h_turn", g)
                if g == 0:
                    need(eng, "xw_mm", n_groups - 1)
                eng.activation(h_cols[:, block_cols(g)], bank[3][:, 0:n], ACT.Copy).then_inc(done("h_cols"), 1)

            def src_rows(g):
                nb = blocks_of[g]
                need(eng, "src_mm", g)
                if g >= 2:
                    loaded(eng, f"src_table{g % 2}", g // 2)
                o = src_out[:, g % 2, 0:nb * 2 * P].rearrange("p (b f) -> p b f", b=nb)[:, :, 0:P]
                eng.activation(o, bank[4][:, 0:nb * P].rearrange("p (b f) -> p b f", b=nb), ACT.Copy).then_inc(done("src_rows"), 1)

            def part(g, k):
                return dst_out[:, g % 2, 0:blocks_of[g] * PARTS * P].rearrange("p (b s f) -> p b s f", s=PARTS, f=P)[:, :, k, :]

            def part0(g):
                nb = blocks_of[g]
                need(eng, "dst_mm", g)
                if g >= 2:
                    loaded(eng, f"dst_table{g % 2}", g // 2)
                eng.activation(part(g, 0), bank[5][:, 0:nb * P].rearrange("p (b f) -> p b f", b=nb), ACT.Copy).then_inc(done("part0"), 1)

            def part1(g):
                nb = blocks_of[g]
                need(eng, "rest", g)
                eng.activation(part(g, 1), rest[:, g % 2, 0:nb * P].rearrange("p (b f) -> p b f", b=nb), ACT.Copy).then_inc(done("part1"), 1)

            run_stages(n_groups, [
                (1, softplus), (2, lambda g: inverse_std(g, "moments1", rstd, moments, "rstd1", "norm1")),
                (3, x1_turned), (4, lambda g: inverse_std(g, "moments2", rstd2, moments2, "rstd2", "norm2")),
                (NORM2_AT, relu), (NORM2_AT + 1, h_turned), (NORM2_AT + 1, src_rows), (NORM2_AT + 1, part0), (NORM2_AT + 2, part1)])

            def hot_turned(c):
                need(eng, "hot_turn", c)
                need(eng, "hidden", c - 2)
                eng.activation(onehot3_t[:, c % 2, :, :], turned(c), ACT.Copy).then_inc(done("hot_t"), 1)

            def edge_weight(c):
                need(eng, "logit", c)
                need(eng, "weigh", c - 4)
                eng.activation(weight[:, c % 4, :], logit[:, c % 4, :], ACT.Sigmoid, bias=be2_all[:, 0:1]).then_inc(done("weight"), 1)

            run_stages(n_chunks, [(1, hot_turned), (3, edge_weight)])

            def far(item, c, start, first):
                eng.wait_ge(done("far_turn"), item)
                eng.activation(onehot3_t[:, 0, :, :], turned(0), ACT.Copy).then_inc(done("far_hot_t"), 1)
                eng.wait_ge(done("far_logit"), item)
                eng.activation(weight[:, 0, :], logit[:, 0, :], ACT.Sigmoid, bias=be2_all[:, 0:1]).then_inc(done("far_weight"), 1)

            further_windows(eng, 1, far)

            for g in range(n_groups):
                n = blocks_of[g] * P
                need(eng, "gate_mm", g)
                need(eng, "mix", g - 2)
                eng.activation(pre[:, g % 2, 0:n], bank[g % 2][:, 0:n], ACT.Sigmoid, bias=bg_col[:, 0:1]).then_inc(done("gate"), 1)
            eng.preload_act_table_set("natural_log_exp_and_others")
            run_stages(n_groups, [
                (0, lambda g: inverse_std(g, "moments3", rstd, moments, "rstd3", "out_norm")),
                (1, lambda g: inverse_std(g, "moments4", rstd2, moments2, "rstd4", "out_rows"))])

        @block.tensor
        def _(eng):
            need(eng, "constants", 0)
            for g in range(row_groups):
                n = min(P, n_chunks - g * P)
                for k in range(2):
                    need(eng, "diag", 2 * g + k)
                    eng.matmul(bank[4 + k][:, g * P:g * P + n], ones[0:n, :], diag[0:n, k, 0:n],
                               start=True, stop=True, skip_group_check=True).then_inc(done("extent_mm"), 1)

            def xw(g):
                nb = blocks_of[g]
                if g == 0:
                    loaded(eng, "x_cols")
                    need(eng, "glob", 0)
                    need(eng, "widest", 0)
                need(eng, "xw", g - 2)
                for b in range(nb):
                    o = bank[4 + g % 2][:, b * P:(b + 1) * P]
                    n0 = (g * GB + b) * P
                    eng.matmul(o, h_cols[:, n0:n0 + P], w_node[:, :], start=True, stop=False)
                    last = eng.matmul(o, glob[:, :], w_glob[:, :], start=False, stop=True)
                last.then_inc(done("xw_mm"), 1)

            for c in range(n_chunks):
                s = c // SUPER
                if c % SUPER == 0:
                    eng.wait_ge(edge_in[s % V_SLOTS], super_ready[s])
                need(eng, "hot", c)
                need(eng, "acc", c - 4)
                edge_sums(eng, edge_out(c), edge_ring[:, s % V_SLOTS, c % SUPER, :, :], onehot[:, c % 4, :, :]).then_inc(done("edge_mm"), 1)
                if c % XW_EVERY == XW_EVERY - 1 and c // XW_EVERY < n_groups:
                    xw(c // XW_EVERY)
            for g in range(n_chunks // XW_EVERY, n_groups):
                xw(g)

            def far_sums(item, c, start, first):
                eng.wait_ge(done("far_edges"), item * 16)
                eng.wait_ge(done("far_hot"), item)
                edge_sums(eng, edge_out(0), edge_ring[:, 0, 0, :, :], onehot[:, 0, :, :]).then_inc(done("far_mm"), 1)

            need(eng, "acc", n_chunks - 1)
            further_windows(eng, 0, far_sums)

            def per_block(g, out, lhs, rhs, row=None, turn=False):
                for b in range(blocks_of[g]):
                    o = out[:, b * P:(b + 1) * P]
                    if turn:
                        last = eng.transpose(o, lhs(b), ident[:, :])
                    else:
                        last = eng.matmul(o, lhs(b), rhs, start=True, stop=row is None)
                        if row is not None:
                            last = eng.matmul(o, ones[0:1, :], row[0:1, :], start=False, stop=True)
                return last

            def mean_mm(g):
                need(eng, "mean", g)
                need(eng, "pre", g - 1)
                per_block(g, bank[0], lambda b: sums[:, 0, (g * GB + b) * P:(g * GB + b + 1) * P], w_edge[:, :]).then_inc(done("mean_mm"), 1)

            def x1_turn(g):
                need(eng, "norm1", g)
                need(eng, "x1_cols", g - 1)
                per_block(g, bank[1], lambda b: x1_rows[:, g * GB + b, :], None, turn=True).then_inc(done("x1_turn"), 1)

            def w1_mm(g):
                need(eng, "x1_cols", g)
                need(eng, "norm2", g - 2)
                per_block(g, w1_bank(g), lambda b: x1_cols[:, g % 2, b * P:(b + 1) * P], w1[:, :], rows["b1"]).then_inc(done("w1_mm"), 1)

            def h_turn(g):
                need(eng, "relu", g)
                need(eng, "h_cols", g - 1)
                per_block(g, bank[3], lambda b: src_out[:, g % 2, b * 2 * P + P:(b + 1) * 2 * P], None, turn=True).then_inc(done("h_turn"), 1)

            def table_mm(g):
                cols = lambda b: h_cols[:, (g * GB + b) * P:(g * GB + b + 1) * P]
                need(eng, "h_cols", g)
                need(eng, "src_rows", g - 1)
                per_block(g, bank[4], cols, we1_src[:, :]).then_inc(done("src_mm"), 1)
                need(eng, "rest", g - 1)
                per_block(g, bank[5], cols, we1_dst[:, :], rows["be1"]).then_inc(done("dst_mm"), 1)

            run_stages(n_groups, [(0, mean_mm), (3, x1_turn), (3, w1_mm), (NORM2_AT, h_turn), (NORM2_AT + 1, table_mm)])

            need(eng, "rest", n_groups - 1)
            need(eng, "src_rows", n_groups - 1)

            def hot_turn(c):
                need(eng, "hot3", c)
                need(eng, "hot_t", c - 2)
                turn_onehot3(eng, turned(c), onehot3[:, c % 3, :, :]).then_inc(done("hot_turn"), 1)

            def hidden_mm(c):
                need(eng, "hot_t", c)
                need(eng, "logit", c - 2)
                eng.wait_ge(window_in[c % Q_SLOTS], 16 * (c // Q_SLOTS + 1))
                dst_part(eng, hidden(c), onehot3_t[:, c % 2, :, :], window[:, c % Q_SLOTS, :]).then_inc(done("hidden"), 1)

            def wsum(c):
                need(eng, "weigh", c)
                need(eng, "acc2", c - 2)
                weighted_sums(eng, window_out(c), gathered[:, c % G_SLOTS, :, :], weighted[:, c % 3, :, :]).then_inc(done("wsum"), 1)

            run_stages(n_chunks, [(0, hot_turn), (2, hidden_mm), (5, wsum)])

            def far(item, c, start, first):
                eng.wait_ge(done("far_hot3"), item)
                turn_onehot3(eng, turned(0), onehot3[:, 0, :, :]).then_inc(done("far_turn"), 1)
                eng.wait_ge(done("far_hot_t"), item)
                eng.wait_ge(done("far_window"), item * 16)
                dst_part(eng, hidden(0), onehot3_t[:, 0, :, :], window[:, 0, :]).then_inc(done("far_hidden"), 1)
                eng.wait_ge(done("far_weigh"), item)
                weighted_sums(eng, window_out(0), gathered[:, 0, :, :], weighted[:, 0, :, :]).then_inc(done("far_wsum"), 1)

            further_windows(eng, 1, far)

            need(eng, "acc2_all", 0)
            for g in range(n_groups):
                n = blocks_of[g] * P
                need(eng, "gate", g - 2)
                eng.matmul(bank[g % 2][:, 0:n], wg_h[:, :], h_cols[:, block_cols(g)], start=True, stop=False)
                eng.matmul(bank[g % 2][:, 0:n], wg_a[:, :], aggr[:, block_cols(g)], start=False, stop=True).then_inc(done("gate_mm"), 1)
            for g in range(n_groups):
                need(eng, "mix", g)
                need(eng, "out_norm", g - 2)
                per_block(g, bank[2 + g % 2], lambda b: aggr[:, (g * GB + b) * P:(g * GB + b + 1) * P], None, turn=True).then_inc(done("mix_turn"), 1)

        @block.vector
        def _(eng):
            own = done("dve")
            made = [0]

            def step(ins):
                made[0] += 1
                ins.then_inc(own, 1)
                eng.wait_ge(own, made[0])

            need(eng, "blank", 2)
            step(eng.tensor_copy(iota3[:, :], iota_i[:, :]))
            step(eng.tensor_copy(iota1[:, :], iota1_i[:, :]))
            eng.tensor_copy(iota3_p, iota_i[:, :])
            step(eng.tensor_copy(iota1_p, iota1_i[:, :]))
            loaded(eng, "chunk_dst", row_groups)
            for g in range(row_groups):
                n = min(P, n_chunks - g * P)
                for k, op in enumerate((ALU.min, ALU.max)):
                    last = eng.tensor_reduce(extent[0:n, g, k:k + 1], chunk_dst[0:n, g, :], AX.X, op)
            last.then_inc(done("extent"), 1)
            need(eng, "extent", 0)
            need(eng, "constants", 0)
            for g in range(row_groups):
                n = min(P, n_chunks - g * P)
                for k in range(2):
                    if g:
                        eng.wait_ge(done("extent_mm"), 2 * (g - 1) + k + 1)
                    eng.tensor_scalar(diag[0:n, k, 0:n], ident[0:n, 0:n], extent[0:n, g, k:k + 1], None, ALU.mult).then_inc(done("diag"), 1)
            eng.wait_ge(done("extent_mm"), 2 * row_groups)
            low, high = bank[4][:, 0:n_chunks], bank[5][:, 0:n_chunks]
            eng.tensor_copy(starts[:, 0:n_chunks], low)
            eng.tensor_copy(start_row[0:1, 0:n_chunks], low[0:1, :])
            eng.tensor_scalar(start3_row[0:1, 0:n_chunks], low[32:33, :], float(PARTS), None, ALU.mult)
            step(eng.tensor_scalar(end_row[0:1, 0:n_chunks], high[64:65, :], 1.0, None, ALU.add))
            step(eng.tensor_tensor(reach[0:1, 0:n_chunks], high[0:1, :], starts[0:1, 0:n_chunks], ALU.subtract))
            step(eng.tensor_reduce(widest[0:1, 0:1], reach[0:1, 0:n_chunks], AX.X, ALU.max))
            eng.tensor_copy(widest_i[0:1, 0:1], widest[0:1, 0:1]).then_inc(done("widest"), 1)
            need(eng, "widest", 0)
            loaded(eng, "lane_dst_i")
            step(eng.tensor_copy(lane_dst[:, :, :], lane_dst_i[:, :, :]))
            step(eng.tensor_tensor(lane_dst[:, :, :], lane_dst[:, :, :],
                                   starts[:, 0:n_chunks].unsqueeze(2).to_broadcast([P, n_chunks, J]), ALU.subtract))
            if repeated:
                step(eng.memset(lane_dst[0:repeated, n_chunks - 1, :], -1.0))
            loaded(eng, "small", N_SMALL)
            eng.tensor_copy(glob[:, :], glob_col[:, 0:1].to_broadcast([64, P])).then_inc(done("glob"), 1)
            need(eng, "zeroed", 0)

            regs = None

            def hot(c):
                need(eng, "edge_mm", c - 4)
                make_onehot(eng, onehot[:, c % 4, :, :], lane_dst[:, c, :]).then_inc(done("hot"), 1)

            def acc(c):
                nonlocal regs
                if c % REGS == 0:
                    regs = load_starts(start_row, c, DVE)
                need(eng, "edge_mm", c)
                need(eng, "acc", c - 1)
                add_window(eng, sums[:, :, :], regs[c % REGS], edge_out(c)).then_inc(done("acc"), 1)

            run_stages(n_chunks, [(0, hot), (2, acc)])

            def far_item(item, c, start, first, dst_out_):
                with eng.If(start < first + (W + 1)):
                    eng.memset(shift[:, :], 0.0).then_inc(done("far_new"), 1)
                eng.drain()
                eng.tensor_scalar(shift[:, :], shift[:, :], float(W), None, ALU.add)
                eng.drain()
                eng.tensor_scalar(dst_out_, lane_dst[:, bass.ds(c, 1), :].rearrange("p a j -> p (a j)"), shift[:, 0:1], None, ALU.subtract)
                eng.drain()

            def far_sums(item, c, start, first):
                far_item(item, c, start, first, far_dst[:, :])
                make_onehot(eng, onehot[:, 0, :, :], far_dst[:, :]).then_inc(done("far_hot"), 1)
                eng.wait_ge(done("far_mm"), item)
                add_window(eng, sums[:, :, :], start, edge_out(0)).then_inc(done("far_acc"), 1)
                eng.wait_ge(done("far_acc"), item + 1)

            need(eng, "acc", n_chunks - 1)
            eng.sem_inc(done("far_acc"), 1)
            further_windows(eng, 0, far_sums)
            eng.sem_inc(done("acc_all"), 1)

            loaded(eng, "x_rows", 2 if tail_nodes else 1)

            def recip(g):
                need(eng, "count", g)
                cols = block_cols(g)
                eng.reciprocal(sums[:, 1, cols], sums[:, 1, cols]).then_inc(done("recip"), 1)

            def pre_(g):
                n = blocks_of[g] * P
                need(eng, "mean_mm", g)
                need(eng, "xw", g)
                need(eng, "soft_sum", g - 2)
                xw = x1_rows[:, g * GB:g * GB + blocks_of[g], :].rearrange("p b f -> p (b f)")
                eng.tensor_tensor(pre[:, g % 2, 0:n], bank[0][:, 0:n], xw, ALU.add).then_inc(done("pre"), 1)

            def soft_sum(g):
                nb = blocks_of[g]
                n = nb * P
                need(eng, "softlog", g)
                t = soft[:, g % 2, 0:n]
                need(eng, "norm1", g - 2)
                y = y1[:, g % 2, 0:n]
                eng.scalar_tensor_tensor(y, pre[:, g % 2, 0:n], 0.0, t, ALU.max, ALU.add).then_inc(done("soft_sum"), 1)
                need(eng, "soft_sum", g)
                xr = x_rows[:, g * GB:g * GB + nb, :].rearrange("p b f -> p (b f)")
                eng.scalar_tensor_tensor(y, y, LN2, xr, ALU.subtract, ALU.add).then_inc(done("res"), 1)
                need(eng, "res", g)
                row_moments(g, y, stats, moments, "rstd1", "moments1")

            def row_moments(g, y, st, mom, used, name):
                nb = blocks_of[g]
                need(eng, used, g - 2)
                for b in range(nb):
                    last = eng.bn_stats(st[:, g % 2, b, :], y[:, b * P:(b + 1) * P])
                last.then_inc(done(name + "_stats"), 1)
                need(eng, name + "_stats", g)
                for b in range(nb):
                    last = eng.bn_aggr(mom[:, g % 2, b, :], st[:, g % 2, b, :])
                last.then_inc(done(name), 1)

            def normalize(g, out, y, rs, mom):
                for b in range(blocks_of[g]):
                    last = eng.tensor_scalar(out(b), y[:, b * P:(b + 1) * P], mom[:, g % 2, b, 0:1], rs[:, g % 2, b:b + 1], ALU.subtract, ALU.mult)
                return last

            def norm1(g):
                need(eng, "rstd1", g)
                normalize(g, lambda b: x1_rows[:, g * GB + b, :], y1[:, g % 2, :], rstd, moments).then_inc(done("norm1"), 1)

            def moments2_(g):
                need(eng, "w1_mm", g)
                row_moments(g, w1_bank(g), stats2, moments2, "rstd2", "moments2")

            def norm2(g):
                need(eng, "rstd2", g)
                need(eng, "relu", g - 2)
                normalize(g, lambda b: z1[:, g % 2, b * P:(b + 1) * P], w1_bank(g), rstd2, moments2).then_inc(done("norm2"), 1)

            def rest_(g):
                nb = blocks_of[g]
                three = dst_out[:, g % 2, 0:nb * PARTS * P].rearrange("p (b s f) -> p b s f", s=PARTS, f=P)
                r = rest[:, g % 2, 0:nb * P].rearrange("p (b f) -> p b f", b=nb)
                need(eng, "part0", g)
                need(eng, "part2", g - 2)
                eng.tensor_tensor(r, bank[5][:, 0:nb * P].rearrange("p (b f) -> p b f", b=nb), three[:, :, 0, :], ALU.subtract).then_inc(done("rest"), 1)

            def part2(g):
                nb = blocks_of[g]
                three = dst_out[:, g % 2, 0:nb * PARTS * P].rearrange("p (b s f) -> p b s f", s=PARTS, f=P)
                r = rest[:, g % 2, 0:nb * P].rearrange("p (b f) -> p b f", b=nb)
                need(eng, "part1", g)
                eng.tensor_tensor(three[:, :, 2, :], r, three[:, :, 1, :], ALU.subtract).then_inc(done("part2"), 1)

            run_stages(n_groups, [(0, recip), (1, pre_), (2, soft_sum), (3, norm1), (4, moments2_), (NORM2_AT, norm2), (NORM2_AT + 1, rest_), (NORM2_AT + 2, part2)])

            need(eng, "mean_mm", n_groups - 1)
            step(eng.memset(aggr, 0.0))

            def hot3(c):
                need(eng, "hot_turn", c - 3)
                make_onehot3(eng, onehot3[:, c % 3, :, :], lane_dst[:, c, :]).then_inc(done("hot3"), 1)

            def src_part(c):
                need(eng, "hidden", c)
                eng.wait_ge(gather_in[c % G_SLOTS], 16 * J * (c // G_SLOTS + 1))
                add_src_part(eng, hidden(c), gathered[:, c % G_SLOTS, :, :]).then_inc(done("hidden_sum"), 1)

            def logits(c):
                need(eng, "hidden_sum", c)
                need(eng, "weight", c - 4)
                edge_dots(eng, logit[:, c % 4, :], hidden(c)).then_inc(done("logit"), 1)

            def weigh_(c):
                need(eng, "weight", c)
                need(eng, "wsum", c - 3)
                weigh(eng, weighted[:, c % 3, :, :], lane_dst[:, c, :], weight[:, c % 4, :]).then_inc(done("weigh"), 1)

            def acc2(c):
                nonlocal regs
                if c % REGS == 0:
                    regs = load_starts(start_row, c, DVE)
                need(eng, "wsum", c)
                need(eng, "acc2", c - 1)
                add_window(eng, aggr, regs[c % REGS], window_out(c)).then_inc(done("acc2"), 1)

            run_stages(n_chunks, [(0, hot3), (4, weigh_), (3, src_part), (3, logits), (6, acc2)])

            def far(item, c, start, first):
                far_item(item, c, start, first, far_dst[:, :])
                make_onehot3(eng, onehot3[:, 0, :, :], far_dst[:, :]).then_inc(done("far_hot3"), 1)
                eng.wait_ge(done("far_token"), item)
                eng.tensor_copy(far_src[:, :], lane_src[:, bass.ds(c * J, J)]).then_inc(done("far_src"), 1)
                eng.wait_ge(done("far_hidden"), item)
                eng.wait_ge(done("far_gather"), item * (16 * J))
                add_src_part(eng, hidden(0), gathered[:, 0, :, :])
                eng.drain()
                edge_dots(eng, logit[:, 0, :], hidden(0)).then_inc(done("far_logit"), 1)
                eng.wait_ge(done("far_weight"), item)
                weigh(eng, weighted[:, 0, :, :], far_dst[:, :], weight[:, 0, :]).then_inc(done("far_weigh"), 1)
                eng.wait_ge(done("far_wsum"), item)
                add_window(eng, aggr, start, window_out(0)).then_inc(done("far_acc2"), 1)
                eng.wait_ge(done("far_acc2"), item + 1)

            need(eng, "acc2", n_chunks - 1)
            eng.sem_inc(done("far_acc2"), 1)
            eng.sem_inc(done("far_token"), 1)
            further_windows(eng, 1, far)
            eng.sem_inc(done("acc2_all"), 1)

            for g in range(n_groups):
                cols = block_cols(g)
                n = blocks_of[g] * P
                d = soft[:, g % 2, 0:n]
                need(eng, "gate_mm", g)
                step(eng.tensor_tensor(d, aggr[:, cols], h_cols[:, cols], ALU.subtract))
                need(eng, "gate", g)
                step(eng.tensor_tensor(d, d, pre[:, g % 2, 0:n], ALU.mult))
                eng.tensor_tensor(aggr[:, cols], d, h_cols[:, cols], ALU.add).then_inc(done("mix"), 1)

            def moments3(g):
                need(eng, "mix_turn", g)
                row_moments(g, bank[2 + g % 2], stats, moments, "rstd3", "moments3")

            def out_norm(g):
                need(eng, "rstd3", g)
                need(eng, "offset2", g - 2)
                need(eng, "res2", g - 2)
                normalize(g, lambda b: z1[:, g % 2, b * P:(b + 1) * P], bank[2 + g % 2], rstd, moments).then_inc(done("out_norm"), 1)

            def residual2(g):
                nb = blocks_of[g]
                n = nb * P
                need(eng, "offset2", g)
                need(eng, "out_rows", g - 2)
                y = x1_cols[:, g % 2, 0:n]
                eng.tensor_tensor(y, z1[:, g % 2, 0:n], x1_rows[:, g * GB:g * GB + nb, :].rearrange("p b f -> p (b f)"), ALU.add).then_inc(done("res2"), 1)
                need(eng, "res2", g)
                row_moments(g, y, stats2, moments2, "rstd4", "moments4")

            def out_rows(g):
                need(eng, "rstd4", g)
                if g >= 2:
                    loaded(eng, f"out{g % 2}", out_dmas(g % 2, g))
                normalize(g, lambda b: y1[:, g % 2, b * P:(b + 1) * P], x1_cols[:, g % 2, :], rstd2, moments2).then_inc(done("out_rows"), 1)

            run_stages(n_groups, [(0, moments3), (1, out_norm), (2, residual2), (3, out_rows)])


N_SMALL = 18
NORM2_AT = 5


def run_stages(n, stages):
    for t in range(n + max(d for d, _ in stages)):
        for d, f in stages:
            if 0 <= t - d < n:
                f(t - d)


def kernel(**inputs):
    import numpy as np
    import concourse.bacc as bacc
    from concourse.bass_utils import run_bass_kernel_spmd

    raw = {k: np.asarray(v) for k, v in inputs.items()}
    n_nodes, n_edges = raw["x"].shape[0], raw["src"].shape[0]

    def by_chunk(a):
        whole = (n_edges - 1) // CHUNK * CHUNK
        return np.concatenate([a[:whole], a[n_edges - CHUNK:]]).reshape(-1, CHUNK)

    def by_lane(a):
        return np.ascontiguousarray(by_chunk(a).reshape(-1, P, J).transpose(1, 0, 2))

    arrays = {
        "x": raw["x"], "x_t": np.ascontiguousarray(raw["x"].T), "edge_attr_128": raw["edge_attr_128"],
        "dst_by_chunk": by_chunk(raw["dst"]), "dst_by_lane": by_lane(raw["dst"]),
        "src_by_lane": by_lane(raw["src"]).reshape(P, -1),
        "L0_gnn_global_feats": raw["L0_gnn_global_feats"], "L0_W_t": np.ascontiguousarray(raw["L0_gnn_W"].T),
    }
    for name in ("W1", "b1", "g1", "bt1", "We1", "be1", "We2", "be2", "Wg", "bg", "g2", "bt2"):
        arrays["L1_gnn_" + name] = raw["L1_gnn_" + name]
    nc = bacc.Bacc("TRN2", target_bir_lowering=False, num_devices=1)
    io = {}
    for name, a in arrays.items():
        io[name] = nc.dram_tensor("in_" + name, a.shape, mybir.dt.from_np(a.dtype), kind="ExternalInput").ap()
    io["out"] = nc.dram_tensor("out_rows", (n_nodes, P), F32, kind="ExternalOutput").ap()
    gnn_pair(nc, n_nodes, n_edges, io)
    r = run_bass_kernel_spmd(nc, [{"in_" + k: np.ascontiguousarray(a) for k, a in arrays.items()}], core_ids=[0])
    return r.results[0]["out_rows"]
```

```python
from contextlib import ExitStack

import concourse.bass as bass
from concourse import mybir

F32 = mybir.dt.float32
BF16 = mybir.dt.bfloat16
I32 = mybir.dt.int32
ALU = mybir.AluOpType
ACT = mybir.ActivationFunctionType
AX = mybir.AxisListType
DVE = mybir.EngineType.DVE
SP = mybir.EngineType.SP

P = 128
J = 4
CHUNK = P * J
W0 = 64
W = 40
PARTS = 3
WP = W * PARTS
REGS = 8
LN_EPS = 1e-5
LN2 = 0.6931471805599453
BANK = 512


def gnn_pair(nc, n_nodes, n_edges, io):
    n_chunks = -(-n_edges // CHUNK)
    last_start = n_edges - CHUNK
    repeated = (n_chunks * CHUNK - n_edges) // J
    n_blocks = -(-n_nodes // P)
    full_blocks = n_nodes // P
    tail_nodes = n_nodes - full_blocks * P
    padded = n_blocks * P
    columns = padded + W0
    dst_rows = padded + W
    n_pairs = -(-n_chunks // 2)
    GB = 4
    n_groups = -(-n_blocks // GB)
    blocks_of = [min(GB, n_blocks - GB * g) for g in range(n_groups)]
    row_groups = -(-n_chunks // P)
    SUPER = 4
    n_supers = -(-n_chunks // SUPER)
    V_SLOTS, G_SLOTS, Q_SLOTS = 4, 6, 4
    SRC_SLOTS = 3

    ctx = ExitStack()
    with ctx:
        def sb(name, shape, dt=F32):
            return ctx.enter_context(nc.sbuf_tensor(name, shape, dt))

        def sem(name):
            return ctx.enter_context(nc.semaphore(name))

        src_table = nc.dram_tensor("src_table", (padded, 2 * P), F32).ap()
        dst_table = nc.dram_tensor("dst_table", (dst_rows * PARTS, P), BF16).ap()

        sums = sb("sums", [P, 2, columns])
        aggr = sums[:, 0, :]
        x_rows = sb("x_rows", [P, n_blocks, P])
        gathered = x_rows[:, :, :].rearrange("p b f -> p (b f)")[:, 0:G_SLOTS * J * 2 * P] \
            .rearrange("p (s j f) -> p s j f", s=G_SLOTS, j=J)
        x1_rows = sb("x1_rows", [P, n_blocks, P])
        h_cols = sb("h_cols", [P, padded])
        ring = sb("ring", [P, 21 * BANK])
        edge_ring = ring[:, 0:V_SLOTS * SUPER * J * P].rearrange("p (s c j f) -> p s c j f", s=V_SLOTS, c=SUPER, j=J)
        x1_flat = x1_rows[:, :, :].rearrange("p b f -> p (b f)")
        early = [0]

        def early_temp(cols):
            early[0] += cols
            assert early[0] <= n_blocks * P
            return x1_flat[:, early[0] - cols:early[0]]

        lane_dst_i = early_temp(n_chunks * J).bitcast(I32).rearrange("p (c j) -> p c j", j=J)
        reach = early_temp(n_chunks)
        chunk_dst = early_temp(row_groups * CHUNK).bitcast(I32).rearrange("p (g e) -> p g e", g=row_groups)
        starts = early_temp(row_groups * P)
        diag = early_temp(2 * P).rearrange("p (k c) -> p k c", k=2)
        chunk_rows = sb("chunk_rows", [P, n_chunks], I32)
        start_row = chunk_rows[0:1, :]
        start3_row = chunk_rows[32:33, :]
        end_row = chunk_rows[64:65, :]
        edge_row = sb("edge_row", [1, n_chunks], I32)
        lane_src = sb("lane_src", [P, n_chunks * J], I32)
        lane_dst = sb("lane_dst", [P, n_chunks, J])
        extent = sb("extent", [P, row_groups, 2])
        widest = sb("widest", [1, 2])
        widest_i = sb("widest_i", [1, 1], I32)
        ident = sb("ident", [P, P])
        ident_b = sb("ident_b", [P, P], BF16)
        ones = sb("ones", [P, P])
        ones_b = sb("ones_b", [P, P], BF16)
        iota_i = sb("iota_i", [P, WP], I32)
        iota1_i = sb("iota1_i", [P, W0], I32)
        iota1 = sb("iota1", [P, W0])
        eps = sb("eps", [P, 1])
        w_node = sb("w_node", [P, P])
        w_edge = sb("w_edge", [P, P])
        w_glob = sb("w_glob", [64, P])
        glob_col = sb("glob_col", [64, 1])
        glob = sb("glob", [64, P])
        w1 = sb("w1", [P, P])
        we1_src = sb("we1_src", [P, P])
        we1_dst = sb("we1_dst", [P, P])
        wg_h = sb("wg_h", [P, P])
        wg_a = sb("wg_a", [P, P])
        bg_col = sb("bg_col", [P, 1])
        be2_all = sb("be2_all", [P, 1])
        behind = ring[0:PARTS, V_SLOTS * SUPER * J * P:]
        bias = behind[:, 0:2 * P].rearrange("p (v f) -> p v f", v=2)
        bias_rest = behind[:, 2 * P:4 * P].rearrange("p (v f) -> p v f", v=2)
        bias_b = behind[:, 4 * P:7 * P].bitcast(BF16).rearrange("p (k v f) -> p k v f", k=PARTS, v=2)
        bias_parts = sb("bias_parts", [PARTS, 2, P], BF16)
        inv_count = sb("inv_count", [P, n_blocks])
        wide = {n: sb(n + "_all", [P, P]) for n in ("g1", "bt1", "we2", "g2", "bt2")}
        onehot = sb("onehot", [P, 4, J, W0])
        pair_rows = sb("pair_rows", [P, 2, P])
        onehot3 = sb("onehot3", [P, 3, J, WP], BF16)
        onehot3_t = sb("onehot3_t", [WP, 2, J, P], BF16)
        window = sb("window", [WP, Q_SLOTS, P], BF16)
        logit = sb("logit", [P, 4, J])
        weight = sb("weight", [P, 4, J])
        weighted = sb("weighted", [P, 3, J, W])
        pad_rows = sb("pad_rows", [WP, P], BF16)
        shift = sb("shift", [P, 1])
        far_dst = sb("far_dst", [P, J])
        far_src = sb("far_src", [P, J], I32)
        far_token = sb("far_token", [P, J], I32)
        stats = sb("stats", [P, 2, GB, 6])
        moments = sb("moments", [P, 2, GB, 2])
        rstd = sb("rstd", [P, 2, GB])
        stats2 = sb("stats2", [P, 2, GB, 6])
        moments2 = sb("moments2", [P, 2, GB, 2])
        rstd2 = sb("rstd2", [P, 2, GB])

        at = [0]

        def temp(cols, dt=F32, depth=2):
            a = ring[:, at[0]:at[0] + cols * depth]
            at[0] += cols * depth
            a = a if dt == F32 else a.bitcast(dt)
            return a.rearrange("p (s c) -> p s c", s=depth)

        GC = GB * P
        pre = temp(GC)
        soft = temp(GC)
        y1 = temp(GC)
        x1_cols = temp(GC)
        z1 = temp(GC)
        rest = temp(GC)
        src_out = temp(2 * GC, depth=SRC_SLOTS)
        dst_out = temp(GC * PARTS // 2, BF16)

        bank = [ctx.enter_context(nc.psum_tensor(f"bank{i}", [P, BANK], F32)) for i in range(8)]
        const_bank = bank[7]
        iota3_p = const_bank[:, 0:WP]
        iota1_p = const_bank[:, 128:128 + W]
        count_out = const_bank[:, 256:256 + n_blocks]

        names = {}

        def done(name):
            if name not in names:
                names[name] = sem("s_" + name)
            return names[name]

        def need(eng, name, n):
            if n >= 0:
                eng.wait_ge(done(name), n + 1)

        def loaded(eng, name, n=1):
            eng.wait_ge(done(name), 16 * n)

        def slot_uses(k, slots):
            return (n_groups - k + slots - 1) // slots

        def whole_blocks(g):
            return blocks_of[g] - (1 if g == n_groups - 1 and tail_nodes else 0)

        def out_dmas(k, end):
            return sum((whole_blocks(g) > 0) + (whole_blocks(g) < blocks_of[g]) for g in range(k, end, 2))

        def block_cols(g):
            return slice(g * GC, g * GC + blocks_of[g] * P)

        def chunk_start(c):
            return min(c * CHUNK, last_start)

        edge_rows = io["edge_attr_128"]

        def edges_of(c, n):
            s = chunk_start(c)
            return edge_rows[s:s + n * CHUNK, :].rearrange("(c p j) f -> p c (j f)", c=n, j=J)

        def super_loads(s):
            first, end = s * SUPER, min((s + 1) * SUPER, n_chunks)
            if end < n_chunks:
                return [(first, end - first)]
            return ([(first, end - 1 - first)] if end - 1 > first else []) + [(end - 1, 1)]

        slot_total = [0] * V_SLOTS
        super_ready = []
        for s in range(n_supers):
            slot_total[s % V_SLOTS] += 16 * len(super_loads(s))
            super_ready.append(slot_total[s % V_SLOTS])
        edge_in = [sem(f"s_edge_in{i}") for i in range(V_SLOTS)]
        gather_in = [sem(f"s_gather_in{i}") for i in range(G_SLOTS)]
        window_in = [sem(f"s_window_in{i}") for i in range(Q_SLOTS)]
        XW_EVERY = 8

        def edge_sums(eng, out, values, hot):
            for j in range(J):
                last = eng.matmul(out, hot[:, j, :], values[:, j, :], start=(j == 0), stop=(j == J - 1), skip_group_check=True)
            return last

        def edge_counts(eng, out, hot):
            half = hot.bitcast(BF16).rearrange("p j (w t) -> p j w t", t=2)
            for j in range(J):
                last = eng.matmul(out, ones_b[:, :], half[:, j, :, 1], start=(j == 0), stop=(j == J - 1), skip_group_check=True)
            return last

        def make_onehot(eng, out, dst):
            return eng.tensor_tensor(out, iota1[:, :].unsqueeze(1).to_broadcast([P, J, W0]),
                                     dst.unsqueeze(2).to_broadcast([P, J, W0]), ALU.is_equal)

        def make_onehot3(eng, out, dst):
            return eng.tensor_tensor(out, iota3_p.unsqueeze(1).to_broadcast([P, J, WP]),
                                     dst.unsqueeze(2).to_broadcast([P, J, WP]), ALU.is_equal)

        def turn_onehot3(eng, out, hot):
            for j in range(J):
                last = eng.transpose(out[:, j, :], hot[:, j, :], ident_b[:, :])
            return last

        def dst_part(eng, out, hot_t, win):
            for j in range(J):
                last = eng.matmul(out[:, j, :], hot_t[:, j, :], win, start=True, stop=True, skip_group_check=True)
            return last

        def add_src_part(eng, out, rows_):
            return eng.tensor_tensor(out, out, rows_[:, :, 0:P], ALU.add)

        def edge_dots(eng, out, hid):
            for j in range(J):
                last = eng.scalar_tensor_tensor(hid[:, j, :], hid[:, j, :], 0.0, wide["we2"][:, :], ALU.max,
                                                ALU.mult, accum_out=out[:, j:j + 1])
            return last

        def weigh(eng, out, dst, wt):
            for j in range(J):
                last = eng.tensor_scalar(out[:, j, :], iota1_p, dst[:, j:j + 1], wt[:, j:j + 1], ALU.is_equal, ALU.mult)
            return last

        def weighted_sums(eng, out, rows_, hot):
            for j in range(J):
                last = eng.matmul(out, rows_[:, j, P:2 * P], hot[:, j, :], start=(j == 0), stop=(j == J - 1))
            return last

        def add_window(eng, table, start, width, part):
            return eng.tensor_tensor(table[..., bass.ds(start, width)], table[..., bass.ds(start, width)], part, ALU.add)

        def load_starts(table, c, engine):
            n = min(REGS, n_chunks - c)
            top = n_nodes - 1 if table is not start3_row else PARTS * (n_nodes - 1)
            _, regs = nc.values_load_multi_w_load_instructions(
                table[0:1, c:c + n], engines=[engine], min_val=0, max_val=top,
                skip_runtime_bounds_check_because="destinations are node numbers")
            return regs

        def further_windows(eng, layer, body):
            width = (W0, W)[layer]
            need(eng, "widest", 0)
            reach_all = eng.value_load(widest_i[0:1, 0:1], min_val=0, max_val=n_nodes - 1)
            with eng.If(reach_all > width - 1):
                count = eng.alloc_register(f"item{layer}")
                eng.reg_mov(count, 0)
                with eng.Fori(0, n_chunks) as c:
                    first = eng.value_load(start_row[0:1, bass.ds(c, 1)], min_val=0, max_val=n_nodes - 1)
                    end = eng.value_load(end_row[0:1, bass.ds(c, 1)], min_val=0, max_val=n_nodes)
                    with eng.If(first + width < end):
                        with eng.Fori(first + width, end, width) as start:
                            eng.reg_add(count, count, 1)
                            body(eng.snap(count, min_val=1, max_val=1 << 20), c, start,
                                 first)

        def w1_bank(g):
            return bank[2 + 4 * (g % 2)]

        def turned(c):
            return bank[c % 2][0:WP, 0:J * P // 2].bitcast(BF16).rearrange("w (j e) -> w j e", j=J)

        def hidden(c):
            return bank[2 + c % 2][:, :].rearrange("p (j f) -> p j f", j=J)

        def window_out(c):
            return bank[4 + c % 2][:, 0:W]

        def pair_sums_of(c):
            return bank[c // 2 % 2][c % 2 * W0:(c % 2 + 1) * W0, 0:P]

        def pair_nodes(q):
            return min(2, n_chunks - 2 * q) * W0

        def pair_out(q):
            return bank[2 + q % 2][:, 0:4 * W0].rearrange("p (t k w) -> p t k w", t=2, k=2)

        block = ctx.enter_context(nc.Block())

        @block.sync
        def _(eng):
            for g in range(row_groups):
                n = min(P, n_chunks - g * P)
                eng.dma_start(chunk_dst[0:n, g, :], io["dst_by_chunk"][g * P:g * P + n, :]).then_inc(done("chunk_dst"), 16)
            eng.dma_start(lane_dst_i[:, :, :], io["dst_by_lane"]).then_inc(done("lane_dst_i"), 16)
            for s in range(n_supers):
                if s >= V_SLOTS:
                    need(eng, "pair_mm", (s - V_SLOTS + 1) * SUPER // 2 - 1)
                for c, n in super_loads(s):
                    k = c - s * SUPER
                    eng.dma_start(edge_ring[:, s % V_SLOTS, k:k + n, :, :].rearrange("p c j f -> p c (j f)"),
                                  edges_of(c, n)).then_inc(edge_in[s % V_SLOTS], 16)

            def far_edges(item, c, start, first):
                row = eng.value_load(edge_row[0:1, bass.ds(c, 1)], min_val=0, max_val=last_start // J)
                eng.wait_ge(done("far_acc"), item)
                eng.dma_start(edge_ring[:, 0, 0, :, :].rearrange("p j f -> p (j f)"),
                              edge_rows.rearrange("(r j) f -> r (j f)", j=J)[bass.ds(row, P), :]).then_inc(done("far_edges"), 16)

            need(eng, "pair_mm", n_pairs - 1)
            need(eng, "edge_row", 0)
            further_windows(eng, 0, far_edges)

            for g in range(n_groups):
                nb = blocks_of[g]
                need(eng, "src_rows", g)
                need(eng, "relu", g)
                eng.dma_start(src_table[g * GC:g * GC + nb * P, :].rearrange("(b p) f -> p b f", p=P),
                              src_out[:, g % SRC_SLOTS, 0:nb * 2 * P].rearrange("p (b f) -> p b f", b=nb)).then_inc(done(f"src_table{g % SRC_SLOTS}"), 16)
                need(eng, "part2", g)
                eng.dma_start(dst_table[g * GC * PARTS:(g * GC + nb * P) * PARTS, :].rearrange("(b p s) f -> p b (s f)", p=P, s=PARTS),
                              dst_out[:, g % 2, 0:nb * PARTS * P].rearrange("p (b f) -> p b f", b=nb)).then_inc(done(f"dst_table{g % 2}"), 16)
            need(eng, "pad_rows", 0)
            eng.dma_start(dst_table[padded * PARTS:dst_rows * PARTS, :], pad_rows[:, :]).then_inc(done("dst_table_pad"), 16)
            loaded(eng, "dst_table_pad")
            for k in range(2):
                loaded(eng, f"dst_table{k}", slot_uses(k, 2))
            for c in range(n_chunks):
                if c % REGS == 0:
                    regs = load_starts(start3_row, c, SP)
                need(eng, "hidden", c - Q_SLOTS)
                eng.dma_start(window[:, c % Q_SLOTS, :], dst_table[bass.ds(regs[c % REGS], WP), :]).then_inc(window_in[c % Q_SLOTS], 16)

            def far_window(item, c, start, first):
                row = eng.snap(start * PARTS, min_val=0, max_val=PARTS * n_nodes)
                eng.wait_ge(done("far_acc2"), item)
                eng.dma_start(window[:, 0, :], dst_table[bass.ds(row, WP), :]).then_inc(done("far_window"), 16)

            need(eng, "hidden", n_chunks - 1)
            further_windows(eng, 1, far_window)

            for g in range(n_groups):
                nb = blocks_of[g]
                need(eng, "out_rows", g)
                full = whole_blocks(g)
                tile = y1[:, g % 2, 0:nb * P].rearrange("p (b f) -> p b f", b=nb)
                if full:
                    eng.dma_start(io["out"][g * GC:g * GC + full * P, :].rearrange("(b p) f -> p b f", p=P),
                                  tile[:, 0:full, :]).then_inc(done(f"out{g % 2}"), 16)
                if full < nb:
                    eng.dma_start(io["out"][full_blocks * P:n_nodes, :], tile[0:tail_nodes, full, :]).then_inc(done(f"out{g % 2}"), 16)
            for k in range(2):
                loaded(eng, f"out{k}", out_dmas(k, n_groups))

        @block.gpsimd
        def _(eng):
            eng.memset(ident[:, :], 0.0).then_inc(done("blank"), 1)
            eng.memset(ident_b[:, :], 0.0).then_inc(done("blank"), 1)
            eng.memset(ones[:, :], 1.0)
            eng.memset(ones_b[:, :], 1.0)
            eng.memset(eps[:, :], LN_EPS)
            eng.memset(shift[:, :], 0.0)
            eng.iota(iota_i[:, :], pattern=[[1, W], [0, PARTS]], base=0, channel_multiplier=0)
            eng.iota(iota1_i[:, :], pattern=[[1, W0]], base=0, channel_multiplier=0)
            eng.iota(edge_row[:, :], pattern=[[P, n_chunks]], base=0, channel_multiplier=0).then_inc(done("blank"), 1)
            need(eng, "blank", 2)
            for m in (ident, ident_b):
                last = eng.affine_select(out=m[:, :], in_=m[:, :], compare_op=ALU.not_equal, fill=1.0, base=0,
                                         pattern=[[-1, P]], channel_multiplier=1)
            last.then_inc(done("constants"), 1)
            eng.tensor_scalar(edge_row[:, :], edge_row[:, :], float(last_start // J), None, ALU.min).then_inc(done("edge_row"), 1)
            eng.memset(pad_rows[:, :], 0.0).then_inc(done("pad_rows"), 1)
            if tail_nodes:
                eng.memset(x_rows[:, full_blocks, :], 0.0)
                eng.memset(h_cols[:, n_nodes:padded], 0.0)
            eng.memset(sums[:, 0, :], 0.0)
            eng.memset(sums[:, 1, :], 0.0).then_inc(done("zeroed"), 1)

            loaded(eng, "x_rows", 2 if tail_nodes else 1)
            eng.tensor_scalar(x_rows[:, :, :], x_rows[:, :, :], LN2, None, ALU.subtract).then_inc(done("x_less"), 1)
            need(eng, "x_less", 0)

            def residual(g):
                nb = blocks_of[g]
                need(eng, "soft_sum", g)
                y = y1[:, g % 2, 0:nb * P]
                xr = x_rows[:, g * GB:g * GB + nb, :].rearrange("p b f -> p (b f)")
                eng.tensor_tensor(y, y, xr, ALU.add).then_inc(done("res"), 1)

            def gain(g):
                nb = blocks_of[g]
                need(eng, "norm2", g)
                z = z1[:, g % 2, 0:nb * P].rearrange("p (b f) -> p b f", b=nb)
                eng.tensor_tensor(z, z, wide["g1"][:, :].unsqueeze(1).to_broadcast([P, nb, P]), ALU.mult).then_inc(done("gain"), 1)
                need(eng, "gain", g)
                eng.tensor_tensor(z, z, wide["bt1"][:, :].unsqueeze(1).to_broadcast([P, nb, P]), ALU.add).then_inc(done("offset"), 1)

            loaded(eng, "small", N_SMALL)
            run_stages(n_groups, [(2, residual), (NORM2_AT, gain)])

            loaded(eng, "lane_src")
            for k in range(min(SRC_SLOTS, n_groups)):
                loaded(eng, f"src_table{k}", slot_uses(k, SRC_SLOTS))
            need(eng, "res", n_groups - 1)
            for c in range(n_chunks):
                need(eng, "wsum", c - G_SLOTS)
                for j in range(J):
                    t = c * J + j
                    eng.indirect_dma_start(gathered[:, c % G_SLOTS, j, :], None, src_table,
                                           bass.IndirectOffsetOnAxis(ap=lane_src[:, t:t + 1], axis=0)).then_inc(gather_in[c % G_SLOTS], 16)

            def far_gather(item, c, start, first):
                eng.wait_ge(done("far_src"), item)
                eng.tensor_tensor(far_token[:, :], far_src[:, :], far_src[:, :], ALU.add).then_inc(done("far_token"), 1)
                for j in range(J):
                    eng.indirect_dma_start(gathered[:, 0, j, :], None, src_table,
                                           bass.IndirectOffsetOnAxis(ap=far_src[:, j:j + 1], axis=0)).then_inc(done("far_gather"), 16)

            need(eng, "wsum", n_chunks - 1)
            further_windows(eng, 1, far_gather)

            def gain2(g):
                nb = blocks_of[g]
                z = z1[:, g % 2, 0:nb * P].rearrange("p (b f) -> p b f", b=nb)
                need(eng, "out_norm", g)
                eng.tensor_tensor(z, z, wide["g2"][:, :].unsqueeze(1).to_broadcast([P, nb, P]), ALU.mult).then_inc(done("gain2"), 1)
                need(eng, "gain2", g)
                eng.tensor_tensor(z, z, wide["bt2"][:, :].unsqueeze(1).to_broadcast([P, nb, P]), ALU.add).then_inc(done("offset2"), 1)

            run_stages(n_groups, [(0, gain2)])

        @block.scalar
        def _(eng):
            def load(dst, src):
                eng.dma_start(dst, src).then_inc(done("small"), 16)

            small = [
                (w_node[:, :], io["L0_W_t"][0:P, :]), (w_edge[:, :], io["L0_W_t"][P:2 * P, :]),
                (w_glob[:, :], io["L0_W_t"][2 * P:2 * P + 64, :]),
                (glob_col[:, :], io["L0_gnn_global_feats"][0:1, :].rearrange("a k -> k a")),
                (w1[:, :], io["L1_gnn_W1"]), (we1_src[:, :], io["L1_gnn_We1"][0:P, :]),
                (we1_dst[:, :], io["L1_gnn_We1"][P:2 * P, :]), (wg_h[:, :], io["L1_gnn_Wg"][0:P, :]),
                (wg_a[:, :], io["L1_gnn_Wg"][P:2 * P, :]),
                (bg_col[:, :], io["L1_gnn_bg"].rearrange("(k a) -> k a", a=1)),
                (be2_all[:, :], io["L1_gnn_be2"].rearrange("(a k) -> a k", a=1).partition_broadcast(P)),
                (bias[:, 0, :], io["L1_gnn_b1"].rearrange("(a k) -> a k", a=1).partition_broadcast(PARTS)),
                (bias[:, 1, :], io["L1_gnn_be1"].rearrange("(a k) -> a k", a=1).partition_broadcast(PARTS)),
                (wide["g1"][:, :], io["L1_gnn_g1"].rearrange("(a k) -> a k", a=1).partition_broadcast(P)),
                (wide["bt1"][:, :], io["L1_gnn_bt1"].rearrange("(a k) -> a k", a=1).partition_broadcast(P)),
                (wide["we2"][:, :], io["L1_gnn_We2"].rearrange("k a -> a k").partition_broadcast(P)),
                (wide["g2"][:, :], io["L1_gnn_g2"].rearrange("(a k) -> a k", a=1).partition_broadcast(P)),
                (wide["bt2"][:, :], io["L1_gnn_bt2"].rearrange("(a k) -> a k", a=1).partition_broadcast(P)),
            ]
            assert len(small) == N_SMALL
            for dst, src in small:
                load(dst, src)
            need(eng, "zeroed", 0)
            eng.dma_start(h_cols[:, 0:n_nodes], io["x_t"]).then_inc(done("x_cols"), 16)
            eng.dma_start(x_rows[:, 0:full_blocks, :], io["x"][0:full_blocks * P, :].rearrange("(b p) f -> p b f", p=P)).then_inc(done("x_rows"), 16)
            if tail_nodes:
                eng.dma_start(x_rows[0:tail_nodes, full_blocks, :], io["x"][full_blocks * P:n_nodes, :]).then_inc(done("x_rows"), 16)
            eng.dma_start(lane_src[:, :], io["src_by_lane"]).then_inc(done("lane_src"), 16)

            eng.preload_act_table_set("natural_log_exp_and_others")

            def xw_out(g):
                nb = blocks_of[g]
                need(eng, "xw_mm", g)
                eng.activation(x1_rows[:, g * GB:g * GB + nb, :].rearrange("p b f -> p (b f)"),
                               bank[4 + g % 2][:, 0:nb * P], ACT.Copy).then_inc(done("xw"), 1)

            for q in range(n_pairs):
                need(eng, "pair_mm", q)
                need(eng, "pair_turn", q - 2)
                r = pair_nodes(q)
                eng.activation(pair_rows[0:r, q % 2, :], bank[q % 2][0:r, 0:P], ACT.Copy).then_inc(done("pair_rows"), 1)
                if q and q % XW_EVERY == 0 and q // XW_EVERY <= n_groups:
                    xw_out(q // XW_EVERY - 1)
            for g in range(min((n_pairs - 1) // XW_EVERY, n_groups), n_groups):
                xw_out(g)

            def far_rows(item, c, start, first):
                eng.wait_ge(done("far_mm"), item)
                eng.activation(pair_rows[0:W0, 0, :], pair_sums_of(0), ACT.Copy).then_inc(done("far_rows"), 1)

            need(eng, "pair_turn", n_pairs - 1)
            further_windows(eng, 0, far_rows)

            def softplus(g):
                n = blocks_of[g] * P
                t = soft[:, g % 2, 0:n]
                need(eng, "pre", g)
                need(eng, "soft_sum", g - 2)
                eng.activation(t, pre[:, g % 2, 0:n], ACT.Abs).then_inc(done("act"), 1)
                eng.wait_ge(done("act"), 2 * g + 1)
                eng.activation(t, t, ACT.Exp, scale=-1.0).then_inc(done("act"), 1)
                eng.wait_ge(done("act"), 2 * g + 2)
                eng.activation(t, t, ACT.Ln, bias=1.0).then_inc(done("softlog"), 1)

            def inverse_std(g, ready, out, mom, name, freed):
                nb = blocks_of[g]
                need(eng, ready, g)
                need(eng, freed, g - 2)
                o = out[:, g % 2, 0:nb]
                eng.activation(o, mom[:, g % 2, 0:nb, 1], ACT.Ln, bias=eps[:, 0:1]).then_inc(done(name + "_ln"), 1)
                need(eng, name + "_ln", g)
                eng.activation(o, o, ACT.Exp, scale=-0.5).then_inc(done(name), 1)

            def x1_turned(g):
                n = blocks_of[g] * P
                need(eng, "x1_turn", g)
                need(eng, "w1_mm", g - 2)
                eng.activation(x1_cols[:, g % 2, 0:n], bank[1][:, 0:n], ACT.Copy).then_inc(done("x1_cols"), 1)

            def relu(g):
                nb = blocks_of[g]
                need(eng, "offset", g)
                if g >= SRC_SLOTS:
                    loaded(eng, f"src_table{g % SRC_SLOTS}", g // SRC_SLOTS)
                o = src_out[:, g % SRC_SLOTS, 0:nb * 2 * P].rearrange("p (b f) -> p b f", b=nb)[:, :, P:2 * P]
                eng.activation(o, z1[:, g % 2, 0:nb * P].rearrange("p (b f) -> p b f", b=nb), ACT.Relu).then_inc(done("relu"), 1)

            def h_turned(g):
                n = blocks_of[g] * P
                need(eng, "h_turn", g)
                if g == 0:
                    need(eng, "xw_mm", n_groups - 1)
                eng.activation(h_cols[:, block_cols(g)], bank[3][:, 0:n], ACT.Copy).then_inc(done("h_cols"), 1)

            def src_rows(g):
                nb = blocks_of[g]
                need(eng, "src_mm", g)
                if g >= SRC_SLOTS:
                    loaded(eng, f"src_table{g % SRC_SLOTS}", g // SRC_SLOTS)
                o = src_out[:, g % SRC_SLOTS, 0:nb * 2 * P].rearrange("p (b f) -> p b f", b=nb)[:, :, 0:P]
                eng.activation(o, bank[4][:, 0:nb * P].rearrange("p (b f) -> p b f", b=nb), ACT.Copy).then_inc(done("src_rows"), 1)

            def part(g, k):
                return dst_out[:, g % 2, 0:blocks_of[g] * PARTS * P].rearrange("p (b s f) -> p b s f", s=PARTS, f=P)[:, :, k, :]

            def part0(g):
                nb = blocks_of[g]
                need(eng, "dst_mm", g)
                if g >= 2:
                    loaded(eng, f"dst_table{g % 2}", g // 2)
                eng.activation(part(g, 0), bank[5][:, 0:nb * P].rearrange("p (b f) -> p b f", b=nb), ACT.Copy).then_inc(done("part0"), 1)

            def part1(g):
                nb = blocks_of[g]
                need(eng, "rest", g)
                eng.activation(part(g, 1), rest[:, g % 2, 0:nb * P].rearrange("p (b f) -> p b f", b=nb), ACT.Copy).then_inc(done("part1"), 1)

            run_stages(n_groups, [
                (NORM2_AT + 2, h_turned), (4, x1_turned), (1, softplus),
                (3, lambda g: inverse_std(g, "moments1", rstd, moments, "rstd1", "norm1")),
                (NORM2_AT + 3, src_rows), (NORM2_AT + 3, part0), (NORM2_AT + 4, part1), (NORM2_AT + 1, relu),
                (5, lambda g: inverse_std(g, "moments2", rstd2, moments2, "rstd2", "norm2"))])

            def hot_turned(c):
                need(eng, "hot_turn", c)
                need(eng, "hidden", c - 2)
                eng.activation(onehot3_t[:, c % 2, :, :], turned(c), ACT.Copy).then_inc(done("hot_t"), 1)

            def edge_weight(c):
                need(eng, "logit", c)
                need(eng, "weigh", c - 4)
                eng.activation(weight[:, c % 4, :], logit[:, c % 4, :], ACT.Sigmoid, bias=be2_all[:, 0:1]).then_inc(done("weight"), 1)

            run_stages(n_chunks, [(1, hot_turned), (3, edge_weight)])

            def far(item, c, start, first):
                eng.wait_ge(done("far_turn"), item)
                eng.activation(onehot3_t[:, 0, :, :], turned(0), ACT.Copy).then_inc(done("far_hot_t"), 1)
                eng.wait_ge(done("far_logit"), item)
                eng.activation(weight[:, 0, :], logit[:, 0, :], ACT.Sigmoid, bias=be2_all[:, 0:1]).then_inc(done("far_weight"), 1)

            further_windows(eng, 1, far)

            for g in range(n_groups):
                n = blocks_of[g] * P
                need(eng, "gate_mm", g)
                need(eng, "mix", g - 2)
                eng.activation(pre[:, g % 2, 0:n], bank[g % 2][:, 0:n], ACT.Sigmoid, bias=bg_col[:, 0:1]).then_inc(done("gate"), 1)
            eng.preload_act_table_set("natural_log_exp_and_others")
            run_stages(n_groups, [
                (0, lambda g: inverse_std(g, "moments3", rstd, moments, "rstd3", "out_norm")),
                (1, lambda g: inverse_std(g, "moments4", rstd2, moments2, "rstd4", "out_rows"))])

        @block.tensor
        def _(eng):
            need(eng, "constants", 0)
            for g in range(row_groups):
                n = min(P, n_chunks - g * P)
                for k in range(2):
                    need(eng, "diag", 2 * g + k)
                    eng.matmul(bank[4 + k][:, g * P:g * P + n], ones[0:n, :], diag[0:n, k, 0:n],
                               start=True, stop=True, skip_group_check=True).then_inc(done("extent_mm"), 1)

            def xw(g):
                nb = blocks_of[g]
                if g == 0:
                    loaded(eng, "x_cols")
                    need(eng, "glob", 0)
                    need(eng, "widest", 0)
                need(eng, "xw", g - 2)
                for b in range(nb):
                    o = bank[4 + g % 2][:, b * P:(b + 1) * P]
                    n0 = (g * GB + b) * P
                    eng.matmul(o, h_cols[:, n0:n0 + P], w_node[:, :], start=True, stop=False)
                    last = eng.matmul(o, glob[:, :], w_glob[:, :], start=False, stop=True)
                last.then_inc(done("xw_mm"), 1)

            def pair_mm(q):
                chunks = range(2 * q, min(2 * q + 2, n_chunks))
                s = 2 * q // SUPER
                if 2 * q % SUPER == 0:
                    eng.wait_ge(edge_in[s % V_SLOTS], super_ready[s])
                need(eng, "hot", q)
                need(eng, "pair_rows", q - 2)
                for c in chunks:
                    edge_sums(eng, pair_sums_of(c), edge_ring[:, s % V_SLOTS, c % SUPER, :, :], onehot[:, c % 4, :, :])
                need(eng, "acc", 2 * (q - 2) + 1)
                for c in chunks:
                    last = edge_counts(eng, pair_out(q)[:, 1, c % 2, :], onehot[:, c % 4, :, :])
                last.then_inc(done("pair_mm"), 1)

            def pair_turn(q):
                need(eng, "pair_rows", q)
                r = pair_nodes(q)
                eng.transpose(bank[2 + q % 2][:, 0:r], pair_rows[0:r, q % 2, :], ident[0:r, 0:r]).then_inc(done("pair_turn"), 1)
                if q % XW_EVERY == XW_EVERY - 1 and q // XW_EVERY < n_groups:
                    xw(q // XW_EVERY)

            run_stages(n_pairs, [(0, pair_mm), (1, pair_turn)])
            for g in range(min(n_pairs // XW_EVERY, n_groups), n_groups):
                xw(g)

            def far_sums(item, c, start, first):
                eng.wait_ge(done("far_edges"), item * 16)
                eng.wait_ge(done("far_hot"), item)
                edge_sums(eng, pair_sums_of(0), edge_ring[:, 0, 0, :, :], onehot[:, 0, :, :])
                edge_counts(eng, pair_out(0)[:, 1, 0, :], onehot[:, 0, :, :]).then_inc(done("far_mm"), 1)
                eng.wait_ge(done("far_rows"), item)
                eng.transpose(bank[2][:, 0:P], pair_rows[:, 0, :], ident[:, :]).then_inc(done("far_turn0"), 1)

            need(eng, "acc", n_chunks - 1)
            further_windows(eng, 0, far_sums)
            need(eng, "acc_all", 0)
            need(eng, "bias_parts", 0)

            for b in range(n_blocks):
                last = eng.matmul(count_out[:, b:b + 1], sums[0:1, 1, b * P:(b + 1) * P], ones[0:1, 0:1],
                                  start=True, stop=True, skip_group_check=True)
            last.then_inc(done("count_mm"), 1)

            def per_block(g, out, lhs, rhs, added=None, turn=False):
                for b in range(blocks_of[g]):
                    o = out[:, b * P:(b + 1) * P]
                    if turn:
                        last = eng.transpose(o, lhs(b), ident[:, :])
                    else:
                        last = eng.matmul(o, lhs(b), rhs, start=True, stop=added is None)
                        if added is not None:
                            last = eng.matmul(o, ones_b[0:PARTS, :], bias_parts[:, added, :], start=False, stop=True)
                return last

            def mean_mm(g):
                need(eng, "pre", g - 1)
                per_block(g, bank[0], lambda b: sums[:, 0, (g * GB + b) * P:(g * GB + b + 1) * P], w_edge[:, :]).then_inc(done("mean_mm"), 1)

            def x1_turn(g):
                need(eng, "norm1", g)
                need(eng, "x1_cols", g - 1)
                per_block(g, bank[1], lambda b: x1_rows[:, g * GB + b, :], None, turn=True).then_inc(done("x1_turn"), 1)

            def w1_mm(g):
                need(eng, "x1_cols", g)
                need(eng, "norm2", g - 2)
                per_block(g, w1_bank(g), lambda b: x1_cols[:, g % 2, b * P:(b + 1) * P], w1[:, :], added=0).then_inc(done("w1_mm"), 1)

            def h_turn(g):
                need(eng, "relu", g)
                need(eng, "h_cols", g - 1)
                per_block(g, bank[3], lambda b: src_out[:, g % SRC_SLOTS, b * 2 * P + P:(b + 1) * 2 * P], None, turn=True).then_inc(done("h_turn"), 1)

            def table_mm(g):
                cols = lambda b: h_cols[:, (g * GB + b) * P:(g * GB + b + 1) * P]
                need(eng, "h_cols", g)
                need(eng, "src_rows", g - 1)
                per_block(g, bank[4], cols, we1_src[:, :]).then_inc(done("src_mm"), 1)
                need(eng, "rest", g - 1)
                per_block(g, bank[5], cols, we1_dst[:, :], added=1).then_inc(done("dst_mm"), 1)

            run_stages(n_groups, [(4, x1_turn), (5, w1_mm), (0, mean_mm), (NORM2_AT + 2, table_mm), (NORM2_AT + 1, h_turn)])

            need(eng, "rest", n_groups - 1)
            need(eng, "src_rows", n_groups - 1)

            def hot_turn(c):
                need(eng, "hot3", c)
                need(eng, "hot_t", c - 2)
                turn_onehot3(eng, turned(c), onehot3[:, c % 3, :, :]).then_inc(done("hot_turn"), 1)

            def hidden_mm(c):
                need(eng, "hot_t", c)
                need(eng, "logit", c - 2)
                eng.wait_ge(window_in[c % Q_SLOTS], 16 * (c // Q_SLOTS + 1))
                dst_part(eng, hidden(c), onehot3_t[:, c % 2, :, :], window[:, c % Q_SLOTS, :]).then_inc(done("hidden"), 1)

            def wsum(c):
                need(eng, "weigh", c)
                need(eng, "acc2", c - 2)
                weighted_sums(eng, window_out(c), gathered[:, c % G_SLOTS, :, :], weighted[:, c % 3, :, :]).then_inc(done("wsum"), 1)

            run_stages(n_chunks, [(0, hot_turn), (2, hidden_mm), (5, wsum)])

            def far(item, c, start, first):
                eng.wait_ge(done("far_hot3"), item)
                turn_onehot3(eng, turned(0), onehot3[:, 0, :, :]).then_inc(done("far_turn"), 1)
                eng.wait_ge(done("far_hot_t"), item)
                eng.wait_ge(done("far_window"), item * 16)
                dst_part(eng, hidden(0), onehot3_t[:, 0, :, :], window[:, 0, :]).then_inc(done("far_hidden"), 1)
                eng.wait_ge(done("far_weigh"), item)
                weighted_sums(eng, window_out(0), gathered[:, 0, :, :], weighted[:, 0, :, :]).then_inc(done("far_wsum"), 1)

            further_windows(eng, 1, far)

            need(eng, "acc2_all", 0)
            for g in range(n_groups):
                n = blocks_of[g] * P
                need(eng, "gate", g - 2)
                eng.matmul(bank[g % 2][:, 0:n], wg_h[:, :], h_cols[:, block_cols(g)], start=True, stop=False)
                eng.matmul(bank[g % 2][:, 0:n], wg_a[:, :], aggr[:, block_cols(g)], start=False, stop=True).then_inc(done("gate_mm"), 1)
            for g in range(n_groups):
                need(eng, "mix", g)
                need(eng, "out_norm", g - 2)
                per_block(g, bank[2 + g % 2], lambda b: aggr[:, (g * GB + b) * P:(g * GB + b + 1) * P], None, turn=True).then_inc(done("mix_turn"), 1)

        @block.vector
        def _(eng):
            own = done("dve")
            made = [0]

            def step(ins):
                made[0] += 1
                ins.then_inc(own, 1)
                eng.wait_ge(own, made[0])

            need(eng, "blank", 2)
            step(eng.tensor_copy(iota1[:, :], iota1_i[:, :]))
            eng.tensor_copy(iota3_p, iota_i[:, :])
            step(eng.tensor_copy(iota1_p, iota1_i[:, 0:W]))
            loaded(eng, "chunk_dst", row_groups)
            for g in range(row_groups):
                n = min(P, n_chunks - g * P)
                for k, op in enumerate((ALU.min, ALU.max)):
                    last = eng.tensor_reduce(extent[0:n, g, k:k + 1], chunk_dst[0:n, g, :], AX.X, op)
            last.then_inc(done("extent"), 1)
            need(eng, "extent", 0)
            need(eng, "constants", 0)
            for g in range(row_groups):
                n = min(P, n_chunks - g * P)
                for k in range(2):
                    if g:
                        eng.wait_ge(done("extent_mm"), 2 * (g - 1) + k + 1)
                    eng.tensor_scalar(diag[0:n, k, 0:n], ident[0:n, 0:n], extent[0:n, g, k:k + 1], None, ALU.mult).then_inc(done("diag"), 1)
            eng.wait_ge(done("extent_mm"), 2 * row_groups)
            low, high = bank[4][:, 0:n_chunks], bank[5][:, 0:n_chunks]
            eng.tensor_copy(starts[:, 0:n_chunks], low)
            eng.tensor_copy(start_row[0:1, 0:n_chunks], low[0:1, :])
            eng.tensor_scalar(start3_row[0:1, 0:n_chunks], low[32:33, :], float(PARTS), None, ALU.mult)
            step(eng.tensor_scalar(end_row[0:1, 0:n_chunks], high[64:65, :], 1.0, None, ALU.add))
            step(eng.tensor_tensor(reach[0:1, 0:n_chunks], high[0:1, :], starts[0:1, 0:n_chunks], ALU.subtract))
            step(eng.tensor_reduce(widest[0:1, 0:1], reach[0:1, 0:n_chunks], AX.X, ALU.max))
            eng.tensor_copy(widest_i[0:1, 0:1], widest[0:1, 0:1]).then_inc(done("widest"), 1)
            need(eng, "widest", 0)
            loaded(eng, "lane_dst_i")
            step(eng.tensor_copy(lane_dst[:, :, :], lane_dst_i[:, :, :]))
            step(eng.tensor_tensor(lane_dst[:, :, :], lane_dst[:, :, :],
                                   starts[:, 0:n_chunks].unsqueeze(2).to_broadcast([P, n_chunks, J]), ALU.subtract))
            if repeated:
                step(eng.memset(lane_dst[0:repeated, n_chunks - 1, :], -1.0))
            loaded(eng, "small", N_SMALL)
            eng.tensor_copy(glob[:, :], glob_col[:, 0:1].to_broadcast([64, P])).then_inc(done("glob"), 1)
            step(eng.tensor_copy(bias_b[:, 0, :, :], bias[:, :, :]))
            step(eng.tensor_tensor(bias_rest[:, :, :], bias[:, :, :], bias_b[:, 0, :, :], ALU.subtract))
            step(eng.tensor_copy(bias_b[:, 1, :, :], bias_rest[:, :, :]))
            step(eng.tensor_tensor(bias_b[:, 2, :, :], bias_rest[:, :, :], bias_b[:, 1, :, :], ALU.subtract))
            step(eng.tensor_scalar(bias_parts[:, :, :], bias_b[:, 0, :, :], ident[0:PARTS, 0:1], None, ALU.mult))
            for k in range(1, PARTS):
                step(eng.scalar_tensor_tensor(bias_parts[:, :, :], bias_b[:, k, :, :], ident[0:PARTS, k:k + 1],
                                              bias_parts[:, :, :], ALU.mult, ALU.add))
            eng.sem_inc(done("bias_parts"), 1)
            need(eng, "zeroed", 0)

            regs = None

            def hot(q):
                need(eng, "pair_mm", q - 2)
                for c in range(2 * q, min(2 * q + 2, n_chunks)):
                    last = make_onehot(eng, onehot[:, c % 4, :, :], lane_dst[:, c, :])
                last.then_inc(done("hot"), 1)

            def acc(q):
                nonlocal regs
                need(eng, "pair_turn", q)
                for c in range(2 * q, min(2 * q + 2, n_chunks)):
                    if c % REGS == 0:
                        regs = load_starts(start_row, c, DVE)
                    need(eng, "acc", c - 1)
                    add_window(eng, sums[:, :, :], regs[c % REGS], W0, pair_out(q)[:, :, c % 2, :]).then_inc(done("acc"), 1)

            run_stages(n_pairs, [(0, hot), (2, acc)])

            def far_item(item, c, start, first, width, dst_out_):
                with eng.If(start < first + (width + 1)):
                    eng.memset(shift[:, :], 0.0).then_inc(done("far_new"), 1)
                eng.drain()
                eng.tensor_scalar(shift[:, :], shift[:, :], float(width), None, ALU.add)
                eng.drain()
                eng.tensor_scalar(dst_out_, lane_dst[:, bass.ds(c, 1), :].rearrange("p a j -> p (a j)"), shift[:, 0:1], None, ALU.subtract)
                eng.drain()

            def far_sums(item, c, start, first):
                far_item(item, c, start, first, W0, far_dst[:, :])
                make_onehot(eng, onehot[:, 0, :, :], far_dst[:, :]).then_inc(done("far_hot"), 1)
                eng.wait_ge(done("far_turn0"), item)
                add_window(eng, sums[:, :, :], start, W0, pair_out(0)[:, :, 0, :]).then_inc(done("far_acc"), 1)
                eng.wait_ge(done("far_acc"), item + 1)

            need(eng, "acc", n_chunks - 1)
            eng.sem_inc(done("far_acc"), 1)
            further_windows(eng, 0, far_sums)
            eng.sem_inc(done("acc_all"), 1)

            need(eng, "count_mm", 0)
            step(eng.tensor_scalar(inv_count[:, :], count_out, 1.0, None, ALU.max))
            step(eng.reciprocal(inv_count[:, :], inv_count[:, :]))

            def pre_(g):
                need(eng, "mean_mm", g)
                need(eng, "xw", g)
                need(eng, "soft_sum", g - 2)
                for b in range(blocks_of[g]):
                    k = g * GB + b
                    last = eng.scalar_tensor_tensor(pre[:, g % 2, b * P:(b + 1) * P], bank[0][:, b * P:(b + 1) * P],
                                                    inv_count[:, k:k + 1], x1_rows[:, k, :], ALU.mult, ALU.add)
                last.then_inc(done("pre"), 1)

            def soft_sum(g):
                nb = blocks_of[g]
                n = nb * P
                need(eng, "softlog", g)
                t = soft[:, g % 2, 0:n]
                need(eng, "norm1", g - 2)
                y = y1[:, g % 2, 0:n]
                eng.scalar_tensor_tensor(y, pre[:, g % 2, 0:n], 0.0, t, ALU.max, ALU.add).then_inc(done("soft_sum"), 1)

            def moments1_(g):
                need(eng, "res", g)
                row_moments(g, y1[:, g % 2, :], stats, moments, "rstd1", "moments1")

            def row_moments(g, y, st, mom, used, name):
                nb = blocks_of[g]
                need(eng, used, g - 2)
                for b in range(nb):
                    last = eng.bn_stats(st[:, g % 2, b, :], y[:, b * P:(b + 1) * P])
                last.then_inc(done(name + "_stats"), 1)
                need(eng, name + "_stats", g)
                for b in range(nb):
                    last = eng.bn_aggr(mom[:, g % 2, b, :], st[:, g % 2, b, :])
                last.then_inc(done(name), 1)

            def normalize(g, out, y, rs, mom):
                for b in range(blocks_of[g]):
                    last = eng.tensor_scalar(out(b), y[:, b * P:(b + 1) * P], mom[:, g % 2, b, 0:1], rs[:, g % 2, b:b + 1], ALU.subtract, ALU.mult)
                return last

            def norm1(g):
                need(eng, "rstd1", g)
                normalize(g, lambda b: x1_rows[:, g * GB + b, :], y1[:, g % 2, :], rstd, moments).then_inc(done("norm1"), 1)

            def moments2_(g):
                need(eng, "w1_mm", g)
                row_moments(g, w1_bank(g), stats2, moments2, "rstd2", "moments2")

            def norm2(g):
                need(eng, "rstd2", g)
                need(eng, "relu", g - 2)
                normalize(g, lambda b: z1[:, g % 2, b * P:(b + 1) * P], w1_bank(g), rstd2, moments2).then_inc(done("norm2"), 1)

            def rest_(g):
                nb = blocks_of[g]
                three = dst_out[:, g % 2, 0:nb * PARTS * P].rearrange("p (b s f) -> p b s f", s=PARTS, f=P)
                r = rest[:, g % 2, 0:nb * P].rearrange("p (b f) -> p b f", b=nb)
                need(eng, "part0", g)
                need(eng, "part2", g - 2)
                eng.tensor_tensor(r, bank[5][:, 0:nb * P].rearrange("p (b f) -> p b f", b=nb), three[:, :, 0, :], ALU.subtract).then_inc(done("rest"), 1)

            def part2(g):
                nb = blocks_of[g]
                three = dst_out[:, g % 2, 0:nb * PARTS * P].rearrange("p (b s f) -> p b s f", s=PARTS, f=P)
                r = rest[:, g % 2, 0:nb * P].rearrange("p (b f) -> p b f", b=nb)
                need(eng, "part1", g)
                eng.tensor_tensor(three[:, :, 2, :], r, three[:, :, 1, :], ALU.subtract).then_inc(done("part2"), 1)

            run_stages(n_groups, [(4, norm1), (1, pre_), (2, soft_sum), (3, moments1_), (NORM2_AT, norm2), (5, moments2_), (NORM2_AT + 3, rest_), (NORM2_AT + 4, part2)])

            need(eng, "mean_mm", n_groups - 1)
            step(eng.memset(aggr, 0.0))

            def hot3(c):
                need(eng, "hot_turn", c - 3)
                make_onehot3(eng, onehot3[:, c % 3, :, :], lane_dst[:, c, :]).then_inc(done("hot3"), 1)

            def src_part(c):
                need(eng, "hidden", c)
                eng.wait_ge(gather_in[c % G_SLOTS], 16 * J * (c // G_SLOTS + 1))
                add_src_part(eng, hidden(c), gathered[:, c % G_SLOTS, :, :]).then_inc(done("hidden_sum"), 1)

            def logits(c):
                need(eng, "hidden_sum", c)
                need(eng, "weight", c - 4)
                edge_dots(eng, logit[:, c % 4, :], hidden(c)).then_inc(done("logit"), 1)

            def weigh_(c):
                need(eng, "weight", c)
                need(eng, "wsum", c - 3)
                weigh(eng, weighted[:, c % 3, :, :], lane_dst[:, c, :], weight[:, c % 4, :]).then_inc(done("weigh"), 1)

            def acc2(c):
                nonlocal regs
                if c % REGS == 0:
                    regs = load_starts(start_row, c, DVE)
                need(eng, "wsum", c)
                need(eng, "acc2", c - 1)
                add_window(eng, aggr, regs[c % REGS], W, window_out(c)).then_inc(done("acc2"), 1)

            run_stages(n_chunks, [(0, hot3), (4, weigh_), (3, src_part), (3, logits), (6, acc2)])

            def far(item, c, start, first):
                far_item(item, c, start, first, W, far_dst[:, :])
                make_onehot3(eng, onehot3[:, 0, :, :], far_dst[:, :]).then_inc(done("far_hot3"), 1)
                eng.wait_ge(done("far_token"), item)
                eng.tensor_copy(far_src[:, :], lane_src[:, bass.ds(c * J, J)]).then_inc(done("far_src"), 1)
                eng.wait_ge(done("far_hidden"), item)
                eng.wait_ge(done("far_gather"), item * (16 * J))
                add_src_part(eng, hidden(0), gathered[:, 0, :, :])
                eng.drain()
                edge_dots(eng, logit[:, 0, :], hidden(0)).then_inc(done("far_logit"), 1)
                eng.wait_ge(done("far_weight"), item)
                weigh(eng, weighted[:, 0, :, :], far_dst[:, :], weight[:, 0, :]).then_inc(done("far_weigh"), 1)
                eng.wait_ge(done("far_wsum"), item)
                add_window(eng, aggr, start, W, window_out(0)).then_inc(done("far_acc2"), 1)
                eng.wait_ge(done("far_acc2"), item + 1)

            need(eng, "acc2", n_chunks - 1)
            eng.sem_inc(done("far_acc2"), 1)
            eng.sem_inc(done("far_token"), 1)
            further_windows(eng, 1, far)
            eng.sem_inc(done("acc2_all"), 1)

            for g in range(n_groups):
                cols = block_cols(g)
                n = blocks_of[g] * P
                d = soft[:, g % 2, 0:n]
                need(eng, "gate_mm", g)
                step(eng.tensor_tensor(d, aggr[:, cols], h_cols[:, cols], ALU.subtract))
                need(eng, "gate", g)
                step(eng.tensor_tensor(d, d, pre[:, g % 2, 0:n], ALU.mult))
                eng.tensor_tensor(aggr[:, cols], d, h_cols[:, cols], ALU.add).then_inc(done("mix"), 1)

            def moments3(g):
                need(eng, "mix_turn", g)
                row_moments(g, bank[2 + g % 2], stats, moments, "rstd3", "moments3")

            def out_norm(g):
                need(eng, "rstd3", g)
                need(eng, "offset2", g - 2)
                need(eng, "res2", g - 2)
                normalize(g, lambda b: z1[:, g % 2, b * P:(b + 1) * P], bank[2 + g % 2], rstd, moments).then_inc(done("out_norm"), 1)

            def residual2(g):
                nb = blocks_of[g]
                n = nb * P
                need(eng, "offset2", g)
                need(eng, "out_rows", g - 2)
                y = x1_cols[:, g % 2, 0:n]
                eng.tensor_tensor(y, z1[:, g % 2, 0:n], x1_rows[:, g * GB:g * GB + nb, :].rearrange("p b f -> p (b f)"), ALU.add).then_inc(done("res2"), 1)
                need(eng, "res2", g)
                row_moments(g, y, stats2, moments2, "rstd4", "moments4")

            def out_rows(g):
                need(eng, "rstd4", g)
                if g >= 2:
                    loaded(eng, f"out{g % 2}", out_dmas(g % 2, g))
                normalize(g, lambda b: y1[:, g % 2, b * P:(b + 1) * P], x1_cols[:, g % 2, :], rstd2, moments2).then_inc(done("out_rows"), 1)

            run_stages(n_groups, [(0, moments3), (1, out_norm), (2, residual2), (3, out_rows)])


N_SMALL = 18
NORM2_AT = 6


def run_stages(n, stages):
    for t in range(n + max(d for d, _ in stages)):
        for d, f in stages:
            if 0 <= t - d < n:
                f(t - d)


def kernel(**inputs):
    import numpy as np
    import concourse.bacc as bacc
    from concourse.bass_utils import run_bass_kernel_spmd

    raw = {k: np.asarray(v) for k, v in inputs.items()}
    n_nodes, n_edges = raw["x"].shape[0], raw["src"].shape[0]

    def by_chunk(a):
        whole = (n_edges - 1) // CHUNK * CHUNK
        return np.concatenate([a[:whole], a[n_edges - CHUNK:]]).reshape(-1, CHUNK)

    def by_lane(a):
        return np.ascontiguousarray(by_chunk(a).reshape(-1, P, J).transpose(1, 0, 2))

    arrays = {
        "x": raw["x"], "x_t": np.ascontiguousarray(raw["x"].T), "edge_attr_128": raw["edge_attr_128"],
        "dst_by_chunk": by_chunk(raw["dst"]), "dst_by_lane": by_lane(raw["dst"]),
        "src_by_lane": by_lane(raw["src"]).reshape(P, -1),
        "L0_gnn_global_feats": raw["L0_gnn_global_feats"], "L0_W_t": np.ascontiguousarray(raw["L0_gnn_W"].T),
    }
    for name in ("W1", "b1", "g1", "bt1", "We1", "be1", "We2", "be2", "Wg", "bg", "g2", "bt2"):
        arrays["L1_gnn_" + name] = raw["L1_gnn_" + name]
    nc = bacc.Bacc("TRN2", target_bir_lowering=False, num_devices=1)
    io = {}
    for name, a in arrays.items():
        io[name] = nc.dram_tensor("in_" + name, a.shape, mybir.dt.from_np(a.dtype), kind="ExternalInput").ap()
    io["out"] = nc.dram_tensor("out_rows", (n_nodes, P), F32, kind="ExternalOutput").ap()
    gnn_pair(nc, n_nodes, n_edges, io)
    r = run_bass_kernel_spmd(nc, [{"in_" + k: np.ascontiguousarray(a) for k, a in arrays.items()}], core_ids=[0])
    return r.results[0]["out_rows"]
```

```python
from contextlib import ExitStack

import concourse.bass as bass
from concourse import mybir

F32 = mybir.dt.float32
BF16 = mybir.dt.bfloat16
I32 = mybir.dt.int32
ALU = mybir.AluOpType
ACT = mybir.ActivationFunctionType
AX = mybir.AxisListType
DVE = mybir.EngineType.DVE
SP = mybir.EngineType.SP

P = 128
J = 4
CHUNK = P * J
W0 = 64
W = 40
PARTS = 3
WP = W * PARTS
REGS = 16
LN_EPS = 1e-5
LN2 = 0.6931471805599453
BANK = 512


def gnn_pair(nc, n_nodes, n_edges, io):
    n_chunks = -(-n_edges // CHUNK)
    last_start = n_edges - CHUNK
    repeated = (n_chunks * CHUNK - n_edges) // J
    n_blocks = -(-n_nodes // P)
    full_blocks = n_nodes // P
    tail_nodes = n_nodes - full_blocks * P
    padded = n_blocks * P
    columns = padded + W0
    dst_rows = padded + W
    n_pairs = -(-n_chunks // 2)
    GB = 4
    n_groups = -(-n_blocks // GB)
    blocks_of = [min(GB, n_blocks - GB * g) for g in range(n_groups)]
    row_groups = -(-n_chunks // P)
    SUPER = 2
    n_supers = -(-n_chunks // SUPER)
    V_SLOTS, G_SLOTS, Q_SLOTS = 8, 6, 4
    SRC_SLOTS, HOT_PAIRS = 3, 3

    ctx = ExitStack()
    with ctx:
        def sb(name, shape, dt=F32):
            return ctx.enter_context(nc.sbuf_tensor(name, shape, dt))

        def sem(name):
            return ctx.enter_context(nc.semaphore(name))

        src_table = nc.dram_tensor("src_table", (padded, 2 * P), F32).ap()
        dst_table = nc.dram_tensor("dst_table", (dst_rows * PARTS, P), BF16).ap()

        sums = sb("sums", [P, 2, columns])
        aggr = sums[:, 0, :]
        gate_h = sums[:, 1, :]
        x_rows = sb("x_rows", [P, n_blocks, P])
        gathered = x_rows[:, :, :].rearrange("p b f -> p (b f)")[:, 0:G_SLOTS * J * 2 * P] \
            .rearrange("p (s j f) -> p s j f", s=G_SLOTS, j=J)
        x1_rows = sb("x1_rows", [P, n_blocks, P])
        h_cols = sb("h_cols", [P, padded])
        ring = sb("ring", [P, 21 * BANK])
        edge_ring = ring[:, 0:V_SLOTS * SUPER * J * P].rearrange("p (s c j f) -> p s c j f", s=V_SLOTS, c=SUPER, j=J)
        x1_flat = x1_rows[:, :, :].rearrange("p b f -> p (b f)")
        early = [0]

        def early_temp(cols):
            early[0] += cols
            assert early[0] <= n_blocks * P
            return x1_flat[:, early[0] - cols:early[0]]

        lane_dst_i = early_temp(n_chunks * J).bitcast(I32).rearrange("p (c j) -> p c j", j=J)
        reach = early_temp(n_chunks)
        chunk_dst = early_temp(row_groups * CHUNK).bitcast(I32).rearrange("p (g e) -> p g e", g=row_groups)
        starts = early_temp(row_groups * P)
        diag = early_temp(2 * P).rearrange("p (k c) -> p k c", k=2)
        chunk_rows = sb("chunk_rows", [P, n_chunks], I32)
        start_row = chunk_rows[0:1, :]
        start3_row = chunk_rows[32:33, :]
        end_row = chunk_rows[64:65, :]
        edge_row = sb("edge_row", [1, n_chunks], I32)
        lane_src = sb("lane_src", [P, n_chunks * J], I32)
        lane_dst = sb("lane_dst", [P, n_chunks, J])
        extent = sb("extent", [P, row_groups, 2])
        widest = sb("widest", [1, 2])
        widest_i = sb("widest_i", [1, 1], I32)
        ident = sb("ident", [P, P])
        ident_b = sb("ident_b", [P, P], BF16)
        ones = sb("ones", [P, P])
        ones_b = sb("ones_b", [P, P], BF16)
        iota_i = sb("iota_i", [P, WP], I32)
        iota1_i = sb("iota1_i", [P, W0], I32)
        iota1 = sb("iota1", [P, W0])
        eps = sb("eps", [P, 1])
        w_node = sb("w_node", [P, P])
        w_edge = sb("w_edge", [P, P])
        w_glob = sb("w_glob", [64, P])
        glob_col = sb("glob_col", [64, 1])
        glob = sb("glob", [64, PARTS])
        w1 = sb("w1", [P, P])
        we1_src = sb("we1_src", [P, P])
        we1_dst = sb("we1_dst", [P, P])
        wg_h = sb("wg_h", [P, P])
        wg_a = sb("wg_a", [P, P])
        bg_col = sb("bg_col", [P, 1])
        be2_all = sb("be2_all", [P, 1])
        bias = early_temp(3 * P)[0:PARTS, :].rearrange("p (v f) -> p v f", v=3)
        bias_rest = early_temp(3 * P)[0:PARTS, :].rearrange("p (v f) -> p v f", v=3)
        bias_b = early_temp(PARTS * 3 * P // 2)[0:PARTS, :].bitcast(BF16).rearrange("p (k v f) -> p k v f", k=PARTS, v=3)
        bias_parts = sb("bias_parts", [PARTS, 3, P], BF16)
        inv_count = sb("inv_count", [P, n_blocks])
        wide = {n: sb(n + "_all", [P, P]) for n in ("g1", "bt1", "we2", "g2", "bt2")}
        behind = ring[:, V_SLOTS * SUPER * J * P:]
        hot_cols = 2 * HOT_PAIRS * J * W0
        onehot = behind[:, 0:hot_cols].rearrange("p (c j w) -> p c j w", c=2 * HOT_PAIRS, j=J)
        pair_rows = behind[:, hot_cols:hot_cols + 2 * P].rearrange("p (q f) -> p q f", q=2)
        onehot3 = sb("onehot3", [P, 3, J, WP], BF16)
        onehot3_t = sb("onehot3_t", [WP, 2, J, P], BF16)
        window = sb("window", [WP, Q_SLOTS, P], BF16)
        logit = sb("logit", [P, 4, J])
        weight = sb("weight", [P, 4, J])
        weighted = sb("weighted", [P, 3, J, W])
        pad_rows = sb("pad_rows", [WP, P], BF16)
        shift = sb("shift", [P, 1])
        far_dst = sb("far_dst", [P, J])
        far_src = sb("far_src", [P, J], I32)
        far_token = sb("far_token", [P, J], I32)
        stats = sb("stats", [P, 2, GB, 6])
        moments = sb("moments", [P, 2, GB, 2])
        rstd = sb("rstd", [P, 2, GB])
        offset = sb("offset", [P, 2, GB])
        stats2 = sb("stats2", [P, 2, GB, 6])
        moments2 = sb("moments2", [P, 2, GB, 2])
        rstd2 = sb("rstd2", [P, 2, GB])

        at = [0]

        def temp(cols, dt=F32, depth=2):
            a = ring[:, at[0]:at[0] + cols * depth]
            at[0] += cols * depth
            a = a if dt == F32 else a.bitcast(dt)
            return a.rearrange("p (s c) -> p s c", s=depth)

        GC = GB * P
        pre = temp(GC)
        soft = temp(GC)
        y1 = temp(GC)
        x1_cols = temp(GC)
        z1 = temp(GC)
        rest = temp(GC)
        assert n_blocks <= P
        moments_all = rest[:, 0, 0:2 * n_blocks].rearrange("p (b t) -> p b t", t=2)
        rstd_all = rest[:, 0, 2 * P:2 * P + n_blocks]
        offset_all = rest[:, 0, 3 * P:3 * P + n_blocks]
        END_SLOTS = SRC_SLOTS
        mix_rows = x_rows
        src_out = temp(2 * GC, depth=SRC_SLOTS)
        last_z = src_out[:, :, 0:GC]
        last_y = src_out[:, :, GC:2 * GC]
        dst_out = temp(GC * PARTS // 2, BF16)

        bank = [ctx.enter_context(nc.psum_tensor(f"bank{i}", [P, BANK], F32)) for i in range(8)]
        const_bank = bank[7]
        iota3_p = const_bank[:, 0:WP]
        iota1_p = const_bank[:, 128:128 + W]
        count_out = const_bank[:, 256:256 + n_blocks]

        names = {}

        def done(name):
            if name not in names:
                names[name] = sem("s_" + name)
            return names[name]

        def need(eng, name, n):
            if n >= 0:
                eng.wait_ge(done(name), n + 1)

        def loaded(eng, name, n=1):
            eng.wait_ge(done(name), 16 * n)

        def slot_uses(k, slots):
            return (n_groups - k + slots - 1) // slots

        def whole_blocks(g):
            return blocks_of[g] - (1 if g == n_groups - 1 and tail_nodes else 0)

        def out_dmas(k, end):
            return sum((whole_blocks(g) > 0) + (whole_blocks(g) < blocks_of[g]) for g in range(k, end, 2))

        def block_cols(g):
            return slice(g * GC, g * GC + blocks_of[g] * P)

        def chunk_start(c):
            return min(c * CHUNK, last_start)

        edge_rows = io["edge_attr_128"]

        def edges_of(c, n):
            s = chunk_start(c)
            return edge_rows[s:s + n * CHUNK, :].rearrange("(c p j) f -> p c (j f)", c=n, j=J)

        def super_loads(s):
            first, end = s * SUPER, min((s + 1) * SUPER, n_chunks)
            if end < n_chunks:
                return [(first, end - first)]
            return ([(first, end - 1 - first)] if end - 1 > first else []) + [(end - 1, 1)]

        slot_total = [0] * V_SLOTS
        super_ready = []
        for s in range(n_supers):
            slot_total[s % V_SLOTS] += 16 * len(super_loads(s))
            super_ready.append(slot_total[s % V_SLOTS])
        edge_in = [sem(f"s_edge_in{i}") for i in range(V_SLOTS)]
        gather_in = [sem(f"s_gather_in{i}") for i in range(G_SLOTS)]
        window_in = [sem(f"s_window_in{i}") for i in range(Q_SLOTS)]
        GROUP_EVERY = 8

        def edge_sums(eng, out, values, hot):
            for j in range(J):
                last = eng.matmul(out, hot[:, j, :], values[:, j, :], start=(j == 0), stop=(j == J - 1), skip_group_check=True)
            return last

        def edge_counts(eng, out, hot):
            half = hot.bitcast(BF16).rearrange("p j (w t) -> p j w t", t=2)
            for j in range(J):
                last = eng.matmul(out, ones_b[:, :], half[:, j, :, 1], start=(j == 0), stop=(j == J - 1), skip_group_check=True)
            return last

        def make_onehot(eng, out, dst):
            return eng.tensor_tensor(out, iota1[:, :].unsqueeze(1).to_broadcast([P, J, W0]),
                                     dst.unsqueeze(2).to_broadcast([P, J, W0]), ALU.is_equal)

        def make_onehot3(eng, out, dst):
            return eng.tensor_tensor(out, iota3_p.unsqueeze(1).to_broadcast([P, J, WP]),
                                     dst.unsqueeze(2).to_broadcast([P, J, WP]), ALU.is_equal)

        def turn_onehot3(eng, out, hot):
            for j in range(J):
                last = eng.transpose(out[:, j, :], hot[:, j, :], ident_b[:, :])
            return last

        def dst_part(eng, out, hot_t, win):
            for j in range(J):
                last = eng.matmul(out[:, j, :], hot_t[:, j, :], win, start=True, stop=True, skip_group_check=True)
            return last

        def add_src_part(eng, out, rows_):
            return eng.tensor_tensor(out, out, rows_[:, :, 0:P], ALU.add)

        def edge_dots(eng, out, hid):
            for j in range(J):
                last = eng.scalar_tensor_tensor(hid[:, j, :], hid[:, j, :], 0.0, wide["we2"][:, :], ALU.max,
                                                ALU.mult, accum_out=out[:, j:j + 1])
            return last

        def weigh(eng, out, dst, wt):
            for j in range(J):
                last = eng.tensor_scalar(out[:, j, :], iota1_p, dst[:, j:j + 1], wt[:, j:j + 1], ALU.is_equal, ALU.mult)
            return last

        def weighted_sums(eng, out, rows_, hot):
            for j in range(J):
                last = eng.matmul(out, rows_[:, j, P:2 * P], hot[:, j, :], start=(j == 0), stop=(j == J - 1))
            return last

        def add_window(eng, table, start, width, part):
            return eng.tensor_tensor(table[..., bass.ds(start, width)], table[..., bass.ds(start, width)], part, ALU.add)

        def load_starts(table, c, engine):
            n = min(REGS, n_chunks - c)
            top = n_nodes - 1 if table is not start3_row else PARTS * (n_nodes - 1)
            _, regs = nc.values_load_multi_w_load_instructions(
                table[0:1, c:c + n], engines=[engine], min_val=0, max_val=top,
                skip_runtime_bounds_check_because="destinations are node numbers")
            return regs

        def further_windows(eng, layer, body):
            width = (W0, W)[layer]
            need(eng, "widest", 0)
            reach_all = eng.value_load(widest_i[0:1, 0:1], min_val=0, max_val=n_nodes - 1)
            with eng.If(reach_all > width - 1):
                count = eng.alloc_register(f"item{layer}")
                eng.reg_mov(count, 0)
                with eng.Fori(0, n_chunks) as c:
                    first = eng.value_load(start_row[0:1, bass.ds(c, 1)], min_val=0, max_val=n_nodes - 1)
                    end = eng.value_load(end_row[0:1, bass.ds(c, 1)], min_val=0, max_val=n_nodes)
                    with eng.If(first + width < end):
                        with eng.Fori(first + width, end, width) as start:
                            eng.reg_add(count, count, 1)
                            body(eng.snap(count, min_val=1, max_val=1 << 20), c, start,
                                 first)

        def w1_bank(g):
            return bank[2 + 4 * (g % 2)]

        def turned(c):
            return bank[c % 2][0:WP, 0:J * P // 2].bitcast(BF16).rearrange("w (j e) -> w j e", j=J)

        def hidden(c):
            return bank[2 + c % 2][:, :].rearrange("p (j f) -> p j f", j=J)

        def window_out(c):
            return bank[4 + c % 2][:, 0:W]

        def pair_sums_of(c):
            return bank[c // 2 % 2][c % 2 * W0:(c % 2 + 1) * W0, 0:P]

        def pair_nodes(q):
            return min(2, n_chunks - 2 * q) * W0

        def pair_bank(q):
            return bank[(2, 3, 6)[q % 3]]

        def pair_out(q):
            return pair_bank(q)[:, 0:4 * W0].rearrange("p (t k w) -> p t k w", t=2, k=2)

        block = ctx.enter_context(nc.Block())

        @block.sync
        def _(eng):
            for g in range(row_groups):
                n = min(P, n_chunks - g * P)
                eng.dma_start(chunk_dst[0:n, g, :], io["dst_by_chunk"][g * P:g * P + n, :]).then_inc(done("chunk_dst"), 16)
            eng.dma_start(lane_dst_i[:, :, :], io["dst_by_lane"]).then_inc(done("lane_dst_i"), 16)
            for s in range(n_supers):
                if s >= V_SLOTS:
                    need(eng, "pair_mm", (s - V_SLOTS + 1) * SUPER // 2 - 1)
                for c, n in super_loads(s):
                    k = c - s * SUPER
                    eng.dma_start(edge_ring[:, s % V_SLOTS, k:k + n, :, :].rearrange("p c j f -> p c (j f)"),
                                  edges_of(c, n)).then_inc(edge_in[s % V_SLOTS], 16)

            def far_edges(item, c, start, first):
                row = eng.value_load(edge_row[0:1, bass.ds(c, 1)], min_val=0, max_val=last_start // J)
                eng.wait_ge(done("far_acc"), item)
                eng.dma_start(edge_ring[:, 0, 0, :, :].rearrange("p j f -> p (j f)"),
                              edge_rows.rearrange("(r j) f -> r (j f)", j=J)[bass.ds(row, P), :]).then_inc(done("far_edges"), 16)

            need(eng, "pair_mm", n_pairs - 1)
            need(eng, "edge_row", 0)
            further_windows(eng, 0, far_edges)

            def src_table_out(g):
                nb = blocks_of[g]
                need(eng, "src_rows", g)
                need(eng, "relu", g)
                eng.dma_start(src_table[g * GC:g * GC + nb * P, :].rearrange("(b p) f -> p b f", p=P),
                              src_out[:, g % SRC_SLOTS, 0:nb * 2 * P].rearrange("p (b f) -> p b f", b=nb)).then_inc(done(f"src_table{g % SRC_SLOTS}"), 16)

            def dst_table_out(g):
                nb = blocks_of[g]
                need(eng, "part2", g)
                eng.dma_start(dst_table[g * GC * PARTS:(g * GC + nb * P) * PARTS, :].rearrange("(b p s) f -> p b (s f)", p=P, s=PARTS),
                              dst_out[:, g % 2, 0:nb * PARTS * P].rearrange("p (b f) -> p b f", b=nb)).then_inc(done(f"dst_table{g % 2}"), 16)
            run_stages(n_groups, [(0, src_table_out), (DST_AT - NORM2_AT - 2, dst_table_out)])
            need(eng, "pad_rows", 0)
            eng.dma_start(dst_table[padded * PARTS:dst_rows * PARTS, :], pad_rows[:, :]).then_inc(done("dst_table_pad"), 16)
            loaded(eng, "dst_table_pad")
            for k in range(2):
                loaded(eng, f"dst_table{k}", slot_uses(k, 2))
            for c in range(n_chunks):
                if c % REGS == 0:
                    regs = load_starts(start3_row, c, SP)
                need(eng, "hidden", c - Q_SLOTS)
                eng.dma_start(window[:, c % Q_SLOTS, :], dst_table[bass.ds(regs[c % REGS], WP), :]).then_inc(window_in[c % Q_SLOTS], 16)

            def far_window(item, c, start, first):
                row = eng.snap(start * PARTS, min_val=0, max_val=PARTS * n_nodes)
                eng.wait_ge(done("far_acc2"), item)
                eng.dma_start(window[:, 0, :], dst_table[bass.ds(row, WP), :]).then_inc(done("far_window"), 16)

            need(eng, "hidden", n_chunks - 1)
            further_windows(eng, 1, far_window)

            for g in range(n_groups):
                nb = blocks_of[g]
                need(eng, "out_rows", g)
                full = whole_blocks(g)
                tile = y1[:, g % 2, 0:nb * P].rearrange("p (b f) -> p b f", b=nb)
                if full:
                    eng.dma_start(io["out"][g * GC:g * GC + full * P, :].rearrange("(b p) f -> p b f", p=P),
                                  tile[:, 0:full, :]).then_inc(done(f"out{g % 2}"), 16)
                if full < nb:
                    eng.dma_start(io["out"][full_blocks * P:n_nodes, :], tile[0:tail_nodes, full, :]).then_inc(done(f"out{g % 2}"), 16)
            for k in range(2):
                loaded(eng, f"out{k}", out_dmas(k, n_groups))

        @block.gpsimd
        def _(eng):
            eng.memset(ident[:, :], 0.0).then_inc(done("blank"), 1)
            eng.memset(ident_b[:, :], 0.0).then_inc(done("blank"), 1)
            eng.memset(ones[:, :], 1.0)
            eng.memset(ones_b[:, :], 1.0)
            eng.memset(eps[:, :], LN_EPS)
            eng.memset(shift[:, :], 0.0)
            eng.iota(iota_i[:, :], pattern=[[1, W], [0, PARTS]], base=0, channel_multiplier=0)
            eng.iota(iota1_i[:, :], pattern=[[1, W0]], base=0, channel_multiplier=0)
            eng.iota(edge_row[:, :], pattern=[[P, n_chunks]], base=0, channel_multiplier=0).then_inc(done("blank"), 1)
            need(eng, "blank", 2)
            for m in (ident, ident_b):
                last = eng.affine_select(out=m[:, :], in_=m[:, :], compare_op=ALU.not_equal, fill=1.0, base=0,
                                         pattern=[[-1, P]], channel_multiplier=1)
            last.then_inc(done("constants"), 1)
            eng.tensor_scalar(edge_row[:, :], edge_row[:, :], float(last_start // J), None, ALU.min).then_inc(done("edge_row"), 1)
            eng.memset(pad_rows[:, :], 0.0).then_inc(done("pad_rows"), 1)
            if tail_nodes:
                eng.memset(x_rows[:, full_blocks, :], 0.0)
                eng.memset(h_cols[:, n_nodes:padded], 0.0)
            eng.memset(sums[:, 0, :], 0.0)
            eng.memset(sums[:, 1, :], 0.0).then_inc(done("zeroed"), 1)

            loaded(eng, "x_rows", 2 if tail_nodes else 1)
            eng.tensor_scalar(x_rows[:, :, :], x_rows[:, :, :], LN2, None, ALU.subtract).then_inc(done("x_less"), 1)
            need(eng, "x_less", 0)

            def residual(g):
                nb = blocks_of[g]
                need(eng, "soft_sum", g)
                y = y1[:, g % 2, 0:nb * P]
                xr = x_rows[:, g * GB:g * GB + nb, :].rearrange("p b f -> p (b f)")
                eng.tensor_tensor(y, y, xr, ALU.add).then_inc(done("res"), 1)

            def gain(g):
                nb = blocks_of[g]
                need(eng, "norm2", g)
                z = z1[:, g % 2, 0:nb * P].rearrange("p (b f) -> p b f", b=nb)
                eng.tensor_tensor(z, z, wide["g1"][:, :].unsqueeze(1).to_broadcast([P, nb, P]), ALU.mult).then_inc(done("gain"), 1)
                need(eng, "gain", g)
                eng.tensor_tensor(z, z, wide["bt1"][:, :].unsqueeze(1).to_broadcast([P, nb, P]), ALU.add).then_inc(done("offset"), 1)

            loaded(eng, "small", N_SMALL)
            run_stages(n_groups, [(2, residual), (NORM2_AT, gain)])

            loaded(eng, "lane_src")
            for k in range(min(SRC_SLOTS, n_groups)):
                loaded(eng, f"src_table{k}", slot_uses(k, SRC_SLOTS))
            need(eng, "res", n_groups - 1)
            for c in range(n_chunks):
                need(eng, "wsum", c - G_SLOTS)
                for j in range(J):
                    t = c * J + j
                    eng.indirect_dma_start(gathered[:, c % G_SLOTS, j, :], None, src_table,
                                           bass.IndirectOffsetOnAxis(ap=lane_src[:, t:t + 1], axis=0)).then_inc(gather_in[c % G_SLOTS], 16)

            def far_gather(item, c, start, first):
                eng.wait_ge(done("far_src"), item)
                eng.tensor_tensor(far_token[:, :], far_src[:, :], far_src[:, :], ALU.add).then_inc(done("far_token"), 1)
                for j in range(J):
                    eng.indirect_dma_start(gathered[:, 0, j, :], None, src_table,
                                           bass.IndirectOffsetOnAxis(ap=far_src[:, j:j + 1], axis=0)).then_inc(done("far_gather"), 16)

            need(eng, "wsum", n_chunks - 1)
            further_windows(eng, 1, far_gather)

            need(eng, "acc2_all", 0)

            def apart(g):
                cols = block_cols(g)
                need(eng, "mix_mul", g - 2)
                eng.tensor_tensor(soft[:, g % 2, 0:blocks_of[g] * P], aggr[:, cols], h_cols[:, cols], ALU.subtract).then_inc(done("apart"), 1)

            def mix_mul(g):
                n = blocks_of[g] * P
                need(eng, "apart", g)
                need(eng, "gate", g)
                need(eng, "mix", g - 2)
                eng.tensor_tensor(y1[:, g % 2, 0:n], soft[:, g % 2, 0:n], pre[:, g % 2, 0:n], ALU.mult).then_inc(done("mix_mul"), 1)

            run_stages(n_groups, [(1, mix_mul), (0, apart)])

            for g in range(n_groups):
                nb = blocks_of[g]
                z = last_z[:, g % END_SLOTS, 0:nb * P].rearrange("p (b f) -> p b f", b=nb)
                need(eng, "out_norm", g)
                eng.tensor_tensor(z, z, wide["g2"][:, :].unsqueeze(1).to_broadcast([P, nb, P]), ALU.mult).then_inc(done("gain2"), 1)
                need(eng, "gain2", g)
                need(eng, "out_rows", g - END_SLOTS)
                need(eng, "x1_offset", g)
                eng.tensor_tensor(last_y[:, g % END_SLOTS, 0:nb * P], last_z[:, g % END_SLOTS, 0:nb * P],
                                  x1_rows[:, g * GB:g * GB + nb, :].rearrange("p b f -> p (b f)"), ALU.add).then_inc(done("res2"), 1)

        @block.scalar
        def _(eng):
            def load(dst, src):
                eng.dma_start(dst, src).then_inc(done("small"), 16)

            small = [
                (w_node[:, :], io["L0_W_t"][0:P, :]), (w_edge[:, :], io["L0_W_t"][P:2 * P, :]),
                (w_glob[:, :], io["L0_W_t"][2 * P:2 * P + 64, :]),
                (glob_col[:, :], io["L0_gnn_global_feats"][0:1, :].rearrange("a k -> k a")),
                (w1[:, :], io["L1_gnn_W1"]), (we1_src[:, :], io["L1_gnn_We1"][0:P, :]),
                (we1_dst[:, :], io["L1_gnn_We1"][P:2 * P, :]), (wg_h[:, :], io["L1_gnn_Wg"][0:P, :]),
                (wg_a[:, :], io["L1_gnn_Wg"][P:2 * P, :]),
                (bg_col[:, :], io["L1_gnn_bg"].rearrange("(k a) -> k a", a=1)),
                (be2_all[:, :], io["L1_gnn_be2"].rearrange("(a k) -> a k", a=1).partition_broadcast(P)),
                (bias[:, 0, :], io["L1_gnn_b1"].rearrange("(a k) -> a k", a=1).partition_broadcast(PARTS)),
                (bias[:, 1, :], io["L1_gnn_be1"].rearrange("(a k) -> a k", a=1).partition_broadcast(PARTS)),
                (wide["g1"][:, :], io["L1_gnn_g1"].rearrange("(a k) -> a k", a=1).partition_broadcast(P)),
                (wide["bt1"][:, :], io["L1_gnn_bt1"].rearrange("(a k) -> a k", a=1).partition_broadcast(P)),
                (wide["we2"][:, :], io["L1_gnn_We2"].rearrange("k a -> a k").partition_broadcast(P)),
                (wide["g2"][:, :], io["L1_gnn_g2"].rearrange("(a k) -> a k", a=1).partition_broadcast(P)),
                (wide["bt2"][:, :], io["L1_gnn_bt2"].rearrange("(a k) -> a k", a=1).partition_broadcast(P)),
            ]
            assert len(small) == N_SMALL
            for dst, src in small:
                load(dst, src)
            need(eng, "zeroed", 0)
            eng.dma_start(h_cols[:, 0:n_nodes], io["x_t"]).then_inc(done("x_cols"), 16)
            eng.dma_start(x_rows[:, 0:full_blocks, :], io["x"][0:full_blocks * P, :].rearrange("(b p) f -> p b f", p=P)).then_inc(done("x_rows"), 16)
            if tail_nodes:
                eng.dma_start(x_rows[0:tail_nodes, full_blocks, :], io["x"][full_blocks * P:n_nodes, :]).then_inc(done("x_rows"), 16)
            eng.dma_start(lane_src[:, :], io["src_by_lane"]).then_inc(done("lane_src"), 16)

            eng.preload_act_table_set("natural_log_exp_and_others")

            def xw_out(g):
                nb = blocks_of[g]
                need(eng, "xw_mm", g)
                eng.activation(x1_rows[:, g * GB:g * GB + nb, :].rearrange("p b f -> p (b f)"),
                               bank[4 + g % 2][:, 0:nb * P], ACT.Copy).then_inc(done("xw"), 1)

            for q in range(n_pairs):
                need(eng, "pair_mm", q)
                need(eng, "pair_turn", q - 2)
                r = pair_nodes(q)
                eng.activation(pair_rows[0:r, q % 2, :], bank[q % 2][0:r, 0:P], ACT.Copy).then_inc(done("pair_rows"), 1)
                if q and q % GROUP_EVERY == 0 and q // GROUP_EVERY <= n_groups:
                    xw_out(q // GROUP_EVERY - 1)
            for g in range(min((n_pairs - 1) // GROUP_EVERY, n_groups), n_groups):
                xw_out(g)

            def far_rows(item, c, start, first):
                eng.wait_ge(done("far_mm"), item)
                eng.activation(pair_rows[0:W0, 0, :], pair_sums_of(0), ACT.Copy).then_inc(done("far_rows"), 1)

            need(eng, "pair_turn", n_pairs - 1)
            further_windows(eng, 0, far_rows)

            def softplus(g):
                n = blocks_of[g] * P
                t = soft[:, g % 2, 0:n]
                need(eng, "pre", g)
                need(eng, "soft_sum", g - 2)
                eng.activation(t, pre[:, g % 2, 0:n], ACT.Abs).then_inc(done("act"), 1)
                eng.wait_ge(done("act"), 2 * g + 1)
                eng.activation(t, t, ACT.Exp, scale=-1.0).then_inc(done("act"), 1)
                eng.wait_ge(done("act"), 2 * g + 2)
                eng.activation(t, t, ACT.Ln, bias=1.0).then_inc(done("softlog"), 1)

            def inverse_std(g, ready, out, mom, name, freed):
                nb = blocks_of[g]
                need(eng, ready, g)
                need(eng, freed, g - 2)
                if freed == "norm1":
                    need(eng, "norm1_act", g - 2)
                o = out[:, g % 2, 0:nb]
                eng.activation(o, mom[:, g % 2, 0:nb, 1], ACT.Ln, bias=eps[:, 0:1]).then_inc(done(name + "_ln"), 1)
                need(eng, name + "_ln", g)
                eng.activation(o, o, ACT.Exp, scale=-0.5).then_inc(done(name), 1)

            def norm1_act(g):
                need(eng, "offset1", g)
                last = None
                for b in range(DVE_BLOCKS, blocks_of[g]):
                    last = eng.activation(x1_rows[:, g * GB + b, :], y1[:, g % 2, b * P:(b + 1) * P], ACT.Identity,
                                          bias=offset[:, g % 2, b:b + 1], scale=rstd[:, g % 2, b:b + 1])
                if last is None:
                    eng.sem_inc(done("norm1_act"), 1)
                else:
                    last.then_inc(done("norm1_act"), 1)

            def x1_turned(g):
                n = blocks_of[g] * P
                need(eng, "x1_turn", g)
                need(eng, "w1_mm", g - 2)
                eng.activation(x1_cols[:, g % 2, 0:n], bank[1][:, 0:n], ACT.Copy).then_inc(done("x1_cols"), 1)

            def relu(g):
                nb = blocks_of[g]
                need(eng, "offset", g)
                if g >= SRC_SLOTS:
                    loaded(eng, f"src_table{g % SRC_SLOTS}", g // SRC_SLOTS)
                o = src_out[:, g % SRC_SLOTS, 0:nb * 2 * P].rearrange("p (b f) -> p b f", b=nb)[:, :, P:2 * P]
                eng.activation(o, z1[:, g % 2, 0:nb * P].rearrange("p (b f) -> p b f", b=nb), ACT.Relu).then_inc(done("relu"), 1)

            def h_turned(g):
                n = blocks_of[g] * P
                need(eng, "h_turn", g)
                if g == 0:
                    need(eng, "xw_mm", n_groups - 1)
                eng.activation(h_cols[:, block_cols(g)], bank[3][:, 0:n], ACT.Copy).then_inc(done("h_cols"), 1)

            def src_rows(g):
                nb = blocks_of[g]
                need(eng, "src_mm", g)
                if g >= SRC_SLOTS:
                    loaded(eng, f"src_table{g % SRC_SLOTS}", g // SRC_SLOTS)
                o = src_out[:, g % SRC_SLOTS, 0:nb * 2 * P].rearrange("p (b f) -> p b f", b=nb)[:, :, 0:P]
                eng.activation(o, bank[4][:, 0:nb * P].rearrange("p (b f) -> p b f", b=nb), ACT.Copy).then_inc(done("src_rows"), 1)

            def part(g, k):
                return dst_out[:, g % 2, 0:blocks_of[g] * PARTS * P].rearrange("p (b s f) -> p b s f", s=PARTS, f=P)[:, :, k, :]

            def part0(g):
                nb = blocks_of[g]
                need(eng, "dst_mm", g)
                if g >= 2:
                    loaded(eng, f"dst_table{g % 2}", g // 2)
                eng.activation(part(g, 0), bank[5][:, 0:nb * P].rearrange("p (b f) -> p b f", b=nb), ACT.Copy).then_inc(done("part0"), 1)

            def part1(g):
                nb = blocks_of[g]
                need(eng, "rest", g)
                eng.activation(part(g, 1), rest[:, g % 2, 0:nb * P].rearrange("p (b f) -> p b f", b=nb), ACT.Copy).then_inc(done("part1"), 1)

            run_stages(n_groups, [
                (4, norm1_act), (NORM2_AT + 2, h_turned), (4, x1_turned), (1, softplus),
                (3, lambda g: inverse_std(g, "moments1", rstd, moments, "rstd1", "norm1")),
                (NORM2_AT + 3, src_rows), (DST_AT + 1, part0), (DST_AT + 2, part1), (NORM2_AT + 1, relu),
                (5, lambda g: inverse_std(g, "moments2", rstd2, moments2, "rstd2", "norm2"))])

            def hot_turned(c):
                need(eng, "hot_turn", c)
                need(eng, "hidden", c - 2)
                eng.activation(onehot3_t[:, c % 2, :, :], turned(c), ACT.Copy).then_inc(done("hot_t"), 1)

            def edge_weight(c):
                need(eng, "logit", c)
                need(eng, "weigh", c - 4)
                eng.activation(weight[:, c % 4, :], logit[:, c % 4, :], ACT.Sigmoid, bias=be2_all[:, 0:1]).then_inc(done("weight"), 1)
                if c % GROUP_EVERY == GROUP_EVERY // 2 and 0 < c // GROUP_EVERY <= n_groups:
                    gate_h_out(c // GROUP_EVERY - 1)

            def gate_h_out(g):
                need(eng, "gate_h_mm", g)
                if g == 0:
                    need(eng, "count_mm", n_groups - 1)
                eng.activation(gate_h[:, block_cols(g)], bank[6][:, 0:blocks_of[g] * P], ACT.Identity, bias=bg_col[:, 0:1]).then_inc(done("gate_h"), 1)

            run_stages(n_chunks, [(1, hot_turned), (3, edge_weight)])
            for g in range(min(max(n_chunks - 1 - GROUP_EVERY // 2, 0) // GROUP_EVERY, n_groups), n_groups):
                gate_h_out(g)

            def far(item, c, start, first):
                eng.wait_ge(done("far_turn"), item)
                eng.activation(onehot3_t[:, 0, :, :], turned(0), ACT.Copy).then_inc(done("far_hot_t"), 1)
                eng.wait_ge(done("far_logit"), item)
                eng.activation(weight[:, 0, :], logit[:, 0, :], ACT.Sigmoid, bias=be2_all[:, 0:1]).then_inc(done("far_weight"), 1)

            further_windows(eng, 1, far)

            def gate(g):
                n = blocks_of[g] * P
                need(eng, "gate_logit", g)
                eng.activation(pre[:, g % 2, 0:n], pre[:, g % 2, 0:n], ACT.Sigmoid).then_inc(done("gate"), 1)

            def mix_out(g):
                nb = blocks_of[g]
                need(eng, "mix_turn", g)
                eng.activation(mix_rows[:, g * GB:g * GB + nb, :].rearrange("p b f -> p (b f)"), bank[2 + g % 2][:, 0:nb * P],
                               ACT.Copy).then_inc(done("mix_rows"), 1)

            run_stages(n_groups, [(0, gate), (3, mix_out)])
            eng.preload_act_table_set("natural_log_exp_and_others")
            need(eng, "moments3", n_groups - 1)
            eng.activation(rstd_all, moments_all[:, :, 1], ACT.Ln, bias=eps[:, 0:1]).then_inc(done("rstd3_ln"), 1)
            need(eng, "rstd3_ln", 0)
            eng.activation(rstd_all, rstd_all, ACT.Exp, scale=-0.5).then_inc(done("rstd3"), 1)
            need(eng, "offset3", 0)

            def out_norm(g):
                need(eng, "mix_rows", g)
                need(eng, "res2", g - END_SLOTS)
                for b in range(blocks_of[g]):
                    k = g * GB + b
                    last = eng.activation(last_z[:, g % END_SLOTS, b * P:(b + 1) * P], mix_rows[:, k, :], ACT.Identity,
                                          bias=offset_all[:, k:k + 1], scale=rstd_all[:, k:k + 1])
                last.then_inc(done("out_norm"), 1)

            run_stages(n_groups, [
                (2, lambda g: inverse_std(g, "moments4", rstd2, moments2, "rstd4", "out_rows")), (0, out_norm)])

        @block.tensor
        def _(eng):
            need(eng, "constants", 0)
            for g in range(row_groups):
                n = min(P, n_chunks - g * P)
                for k in range(2):
                    need(eng, "diag", 2 * g + k)
                    eng.matmul(bank[4 + k][:, g * P:g * P + n], ones[0:n, :], diag[0:n, k, 0:n],
                               start=True, stop=True, skip_group_check=True).then_inc(done("extent_mm"), 1)

            loaded(eng, "small", N_SMALL)
            need(eng, "glob", 0)
            eng.matmul(bank[4][0:PARTS, 0:P], glob[:, :], w_glob[:, :], start=True, stop=True,
                       skip_group_check=True).then_inc(done("glob_mm"), 1)

            def xw(g):
                nb = blocks_of[g]
                if g == 0:
                    loaded(eng, "x_cols")
                    need(eng, "bias_parts", 0)
                need(eng, "xw", g - 2)
                for b in range(nb):
                    o = bank[4 + g % 2][:, b * P:(b + 1) * P]
                    n0 = (g * GB + b) * P
                    eng.matmul(o, h_cols[:, n0:n0 + P], w_node[:, :], start=True, stop=False)
                    last = eng.matmul(o, ones_b[0:PARTS, :], bias_parts[:, 2, :], start=False, stop=True)
                last.then_inc(done("xw_mm"), 1)

            def pair_mm(q):
                chunks = range(2 * q, min(2 * q + 2, n_chunks))
                s = 2 * q // SUPER
                if 2 * q % SUPER == 0:
                    eng.wait_ge(edge_in[s % V_SLOTS], super_ready[s])
                need(eng, "hot", q)
                need(eng, "pair_rows", q - 2)
                for c in chunks:
                    edge_sums(eng, pair_sums_of(c), edge_ring[:, s % V_SLOTS, c % SUPER, :, :], onehot[:, c % (2 * HOT_PAIRS), :, :])
                need(eng, "acc", 2 * (q - 3) + 1)
                for c in chunks:
                    last = edge_counts(eng, pair_out(q)[:, 1, c % 2, :], onehot[:, c % (2 * HOT_PAIRS), :, :])
                last.then_inc(done("pair_mm"), 1)

            def pair_turn(q):
                need(eng, "pair_rows", q)
                r = pair_nodes(q)
                eng.transpose(pair_bank(q)[:, 0:r], pair_rows[0:r, q % 2, :], ident[0:r, 0:r]).then_inc(done("pair_turn"), 1)
                if q % GROUP_EVERY == GROUP_EVERY - 1 and q // GROUP_EVERY < n_groups:
                    xw(q // GROUP_EVERY)

            run_stages(n_pairs, [(0, pair_mm), (1, pair_turn)])
            for g in range(min(n_pairs // GROUP_EVERY, n_groups), n_groups):
                xw(g)

            def far_sums(item, c, start, first):
                eng.wait_ge(done("far_edges"), item * 16)
                eng.wait_ge(done("far_hot"), item)
                edge_sums(eng, pair_sums_of(0), edge_ring[:, 0, 0, :, :], onehot[:, 0, :, :])
                edge_counts(eng, pair_out(0)[:, 1, 0, :], onehot[:, 0, :, :]).then_inc(done("far_mm"), 1)
                eng.wait_ge(done("far_rows"), item)
                eng.transpose(pair_bank(0)[:, 0:P], pair_rows[:, 0, :], ident[:, :]).then_inc(done("far_turn0"), 1)

            need(eng, "acc", n_chunks - 1)
            further_windows(eng, 0, far_sums)
            need(eng, "acc_all", 0)

            def per_block(g, out, lhs, rhs, added=None, turn=False):
                for b in range(blocks_of[g]):
                    o = out[:, b * P:(b + 1) * P]
                    if turn:
                        last = eng.transpose(o, lhs(b), ident[:, :])
                    else:
                        last = eng.matmul(o, lhs(b), rhs, start=True, stop=added is None)
                        if added is not None:
                            last = eng.matmul(o, ones_b[0:PARTS, :], bias_parts[:, added, :], start=False, stop=True)
                return last

            def mean_mm(g):
                need(eng, "pre", g - 1)
                for b in range(g * GB, g * GB + blocks_of[g]):
                    last = eng.matmul(count_out[:, b:b + 1], sums[0:1, 1, b * P:(b + 1) * P], ones[0:1, 0:1],
                                      start=True, stop=True, skip_group_check=True)
                last.then_inc(done("count_mm"), 1)
                per_block(g, bank[0], lambda b: sums[:, 0, (g * GB + b) * P:(g * GB + b + 1) * P], w_edge[:, :]).then_inc(done("mean_mm"), 1)

            def x1_turn(g):
                need(eng, "norm1", g)
                need(eng, "norm1_act", g)
                need(eng, "x1_cols", g - 1)
                per_block(g, bank[1], lambda b: x1_rows[:, g * GB + b, :], None, turn=True).then_inc(done("x1_turn"), 1)

            def w1_mm(g):
                need(eng, "x1_cols", g)
                need(eng, "norm2", g - 2)
                per_block(g, w1_bank(g), lambda b: x1_cols[:, g % 2, b * P:(b + 1) * P], w1[:, :], added=0).then_inc(done("w1_mm"), 1)

            def h_turn(g):
                need(eng, "relu", g)
                need(eng, "h_cols", g - 1)
                per_block(g, bank[3], lambda b: src_out[:, g % SRC_SLOTS, b * 2 * P + P:(b + 1) * 2 * P], None, turn=True).then_inc(done("h_turn"), 1)

            def h_block(g, b):
                return h_cols[:, (g * GB + b) * P:(g * GB + b + 1) * P]

            def src_mm(g):
                need(eng, "h_cols", g)
                need(eng, "src_rows", g - 1)
                per_block(g, bank[4], lambda b: h_block(g, b), we1_src[:, :]).then_inc(done("src_mm"), 1)

            def dst_mm(g):
                need(eng, "rest", g - 1)
                per_block(g, bank[5], lambda b: h_block(g, b), we1_dst[:, :], added=1).then_inc(done("dst_mm"), 1)

            run_stages(n_groups, [
                (4, x1_turn), (5, w1_mm), (0, mean_mm), (NORM2_AT + 2, src_mm), (NORM2_AT + 1, h_turn), (DST_AT, dst_mm)])

            need(eng, "rest", n_groups - 1)
            need(eng, "src_rows", n_groups - 1)

            def hot_turn(c):
                need(eng, "hot3", c)
                need(eng, "hot_t", c - 2)
                turn_onehot3(eng, turned(c), onehot3[:, c % 3, :, :]).then_inc(done("hot_turn"), 1)

            def hidden_mm(c):
                need(eng, "hot_t", c)
                need(eng, "logit", c - 2)
                eng.wait_ge(window_in[c % Q_SLOTS], 16 * (c // Q_SLOTS + 1))
                dst_part(eng, hidden(c), onehot3_t[:, c % 2, :, :], window[:, c % Q_SLOTS, :]).then_inc(done("hidden"), 1)

            def wsum(c):
                need(eng, "weigh", c)
                need(eng, "acc2", c - 2)
                weighted_sums(eng, window_out(c), gathered[:, c % G_SLOTS, :, :], weighted[:, c % 3, :, :]).then_inc(done("wsum"), 1)
                if c % GROUP_EVERY == GROUP_EVERY - 1 and c // GROUP_EVERY < n_groups:
                    gate_h_mm(c // GROUP_EVERY)

            def gate_h_mm(g):
                need(eng, "gate_h", g - 1)
                eng.matmul(bank[6][:, 0:blocks_of[g] * P], wg_h[:, :], h_cols[:, block_cols(g)], start=True, stop=True).then_inc(done("gate_h_mm"), 1)

            run_stages(n_chunks, [(0, hot_turn), (2, hidden_mm), (5, wsum)])
            for g in range(min(n_chunks // GROUP_EVERY, n_groups), n_groups):
                gate_h_mm(g)

            def far(item, c, start, first):
                eng.wait_ge(done("far_hot3"), item)
                turn_onehot3(eng, turned(0), onehot3[:, 0, :, :]).then_inc(done("far_turn"), 1)
                eng.wait_ge(done("far_hot_t"), item)
                eng.wait_ge(done("far_window"), item * 16)
                dst_part(eng, hidden(0), onehot3_t[:, 0, :, :], window[:, 0, :]).then_inc(done("far_hidden"), 1)
                eng.wait_ge(done("far_weigh"), item)
                weighted_sums(eng, window_out(0), gathered[:, 0, :, :], weighted[:, 0, :, :]).then_inc(done("far_wsum"), 1)

            further_windows(eng, 1, far)

            need(eng, "acc2_all", 0)

            def gate_mm(g):
                n = blocks_of[g] * P
                need(eng, "gate_logit", g - 2)
                eng.matmul(bank[g % 2][:, 0:n], wg_a[:, :], aggr[:, block_cols(g)], start=True, stop=True).then_inc(done("gate_mm"), 1)

            def mix_turn(g):
                need(eng, "mix", g)
                need(eng, "mix_rows", g - 2)
                per_block(g, bank[2 + g % 2], lambda b: aggr[:, (g * GB + b) * P:(g * GB + b + 1) * P], None, turn=True).then_inc(done("mix_turn"), 1)

            run_stages(n_groups, [(0, gate_mm), (3, mix_turn)])

        @block.vector
        def _(eng):
            own = done("dve")
            made = [0]

            def step(ins):
                made[0] += 1
                ins.then_inc(own, 1)
                eng.wait_ge(own, made[0])

            need(eng, "blank", 2)
            step(eng.tensor_copy(iota1[:, :], iota1_i[:, :]))
            eng.tensor_copy(iota3_p, iota_i[:, :])
            step(eng.tensor_copy(iota1_p, iota1_i[:, 0:W]))
            loaded(eng, "chunk_dst", row_groups)
            for g in range(row_groups):
                n = min(P, n_chunks - g * P)
                for k, op in enumerate((ALU.min, ALU.max)):
                    last = eng.tensor_reduce(extent[0:n, g, k:k + 1], chunk_dst[0:n, g, :], AX.X, op)
            last.then_inc(done("extent"), 1)
            need(eng, "extent", 0)
            need(eng, "constants", 0)
            for g in range(row_groups):
                n = min(P, n_chunks - g * P)
                for k in range(2):
                    if g:
                        eng.wait_ge(done("extent_mm"), 2 * (g - 1) + k + 1)
                    eng.tensor_scalar(diag[0:n, k, 0:n], ident[0:n, 0:n], extent[0:n, g, k:k + 1], None, ALU.mult).then_inc(done("diag"), 1)
            eng.wait_ge(done("extent_mm"), 2 * row_groups)
            low, high = bank[4][:, 0:n_chunks], bank[5][:, 0:n_chunks]
            eng.tensor_copy(starts[:, 0:n_chunks], low)
            eng.tensor_copy(start_row[0:1, 0:n_chunks], low[0:1, :])
            eng.tensor_scalar(start3_row[0:1, 0:n_chunks], low[32:33, :], float(PARTS), None, ALU.mult)
            step(eng.tensor_scalar(end_row[0:1, 0:n_chunks], high[64:65, :], 1.0, None, ALU.add))
            step(eng.tensor_tensor(reach[0:1, 0:n_chunks], high[0:1, :], starts[0:1, 0:n_chunks], ALU.subtract))
            step(eng.tensor_reduce(widest[0:1, 0:1], reach[0:1, 0:n_chunks], AX.X, ALU.max))
            eng.tensor_copy(widest_i[0:1, 0:1], widest[0:1, 0:1]).then_inc(done("widest"), 1)
            need(eng, "widest", 0)
            loaded(eng, "lane_dst_i")
            step(eng.tensor_copy(lane_dst[:, :, :], lane_dst_i[:, :, :]))
            step(eng.tensor_tensor(lane_dst[:, :, :], lane_dst[:, :, :],
                                   starts[:, 0:n_chunks].unsqueeze(2).to_broadcast([P, n_chunks, J]), ALU.subtract))
            if repeated:
                step(eng.memset(lane_dst[0:repeated, n_chunks - 1, :], -1.0))
            loaded(eng, "small", N_SMALL)
            eng.tensor_copy(glob[:, :], glob_col[:, 0:1].to_broadcast([64, PARTS])).then_inc(done("glob"), 1)
            need(eng, "glob_mm", 0)
            step(eng.tensor_copy(bias[:, 2, :], bank[4][0:PARTS, 0:P]))
            step(eng.tensor_copy(bias_b[:, 0, :, :], bias[:, :, :]))
            step(eng.tensor_tensor(bias_rest[:, :, :], bias[:, :, :], bias_b[:, 0, :, :], ALU.subtract))
            step(eng.tensor_copy(bias_b[:, 1, :, :], bias_rest[:, :, :]))
            step(eng.tensor_tensor(bias_b[:, 2, :, :], bias_rest[:, :, :], bias_b[:, 1, :, :], ALU.subtract))
            step(eng.tensor_scalar(bias_parts[:, :, :], bias_b[:, 0, :, :], ident[0:PARTS, 0:1], None, ALU.mult))
            for k in range(1, PARTS):
                step(eng.scalar_tensor_tensor(bias_parts[:, :, :], bias_b[:, k, :, :], ident[0:PARTS, k:k + 1],
                                              bias_parts[:, :, :], ALU.mult, ALU.add))
            eng.sem_inc(done("bias_parts"), 1)
            need(eng, "zeroed", 0)

            regs = None

            def hot(q):
                need(eng, "pair_mm", q - HOT_PAIRS)
                for c in range(2 * q, min(2 * q + 2, n_chunks)):
                    last = make_onehot(eng, onehot[:, c % (2 * HOT_PAIRS), :, :], lane_dst[:, c, :])
                last.then_inc(done("hot"), 1)

            def acc(q):
                nonlocal regs
                need(eng, "pair_turn", q)
                for c in range(2 * q, min(2 * q + 2, n_chunks)):
                    if c % REGS == 0:
                        regs = load_starts(start_row, c, DVE)
                    need(eng, "acc", c - 1)
                    add_window(eng, sums[:, :, :], regs[c % REGS], W0, pair_out(q)[:, :, c % 2, :]).then_inc(done("acc"), 1)

            run_stages(n_pairs, [(0, hot), (3, acc)])

            def far_item(item, c, start, first, width, dst_out_):
                with eng.If(start < first + (width + 1)):
                    eng.memset(shift[:, :], 0.0).then_inc(done("far_new"), 1)
                eng.drain()
                eng.tensor_scalar(shift[:, :], shift[:, :], float(width), None, ALU.add)
                eng.drain()
                eng.tensor_scalar(dst_out_, lane_dst[:, bass.ds(c, 1), :].rearrange("p a j -> p (a j)"), shift[:, 0:1], None, ALU.subtract)
                eng.drain()

            def far_sums(item, c, start, first):
                far_item(item, c, start, first, W0, far_dst[:, :])
                make_onehot(eng, onehot[:, 0, :, :], far_dst[:, :]).then_inc(done("far_hot"), 1)
                eng.wait_ge(done("far_turn0"), item)
                add_window(eng, sums[:, :, :], start, W0, pair_out(0)[:, :, 0, :]).then_inc(done("far_acc"), 1)
                eng.wait_ge(done("far_acc"), item + 1)

            need(eng, "acc", n_chunks - 1)
            eng.sem_inc(done("far_acc"), 1)
            further_windows(eng, 0, far_sums)
            eng.sem_inc(done("acc_all"), 1)

            def pre_(g):
                need(eng, "count_mm", g)
                some = slice(g * GB, g * GB + blocks_of[g])
                step(eng.tensor_scalar(inv_count[:, some], count_out[:, some], 1.0, None, ALU.max))
                step(eng.reciprocal(inv_count[:, some], inv_count[:, some]))
                need(eng, "mean_mm", g)
                need(eng, "xw", g)
                need(eng, "soft_sum", g - 2)
                for b in range(blocks_of[g]):
                    k = g * GB + b
                    last = eng.scalar_tensor_tensor(pre[:, g % 2, b * P:(b + 1) * P], bank[0][:, b * P:(b + 1) * P],
                                                    inv_count[:, k:k + 1], x1_rows[:, k, :], ALU.mult, ALU.add)
                last.then_inc(done("pre"), 1)

            def soft_sum(g):
                nb = blocks_of[g]
                n = nb * P
                need(eng, "softlog", g)
                t = soft[:, g % 2, 0:n]
                need(eng, "norm1", g - 2)
                need(eng, "norm1_act", g - 2)
                y = y1[:, g % 2, 0:n]
                eng.scalar_tensor_tensor(y, pre[:, g % 2, 0:n], 0.0, t, ALU.max, ALU.add).then_inc(done("soft_sum"), 1)

            def moments1_(g):
                need(eng, "res", g)
                row_moments(g, y1[:, g % 2, :], stats, moments, "rstd1", "moments1")

            def bn_moments(g, y, st, out, name):
                nb = blocks_of[g]
                for b in range(nb):
                    last = eng.bn_stats(st[:, g % 2, b, :], y[:, b * P:(b + 1) * P])
                last.then_inc(done(name + "_stats"), 1)
                need(eng, name + "_stats", g)
                for b in range(nb):
                    last = eng.bn_aggr(out[:, b, :], st[:, g % 2, b, :])
                last.then_inc(done(name), 1)

            def row_moments(g, y, st, mom, used, name):
                need(eng, used, g - 2)
                bn_moments(g, y, st, mom[:, g % 2, :, :], name)

            def normalize(g, out, y, rs, mom, blocks=GB):
                for b in range(min(blocks, blocks_of[g])):
                    last = eng.tensor_scalar(out(b), y[:, b * P:(b + 1) * P], mom[:, g % 2, b, 0:1], rs[:, g % 2, b:b + 1], ALU.subtract, ALU.mult)
                return last

            def norm1(g):
                nb = blocks_of[g]
                need(eng, "rstd1", g)
                need(eng, "norm1_act", g - 2)
                eng.scalar_tensor_tensor(offset[:, g % 2, 0:nb], moments[:, g % 2, 0:nb, 0], -1.0, rstd[:, g % 2, 0:nb],
                                         ALU.mult, ALU.mult).then_inc(done("offset1"), 1)
                normalize(g, lambda b: x1_rows[:, g * GB + b, :], y1[:, g % 2, :], rstd, moments, DVE_BLOCKS).then_inc(done("norm1"), 1)

            def moments2_(g):
                need(eng, "w1_mm", g)
                row_moments(g, w1_bank(g), stats2, moments2, "rstd2", "moments2")

            def norm2(g):
                need(eng, "rstd2", g)
                need(eng, "relu", g - 2)
                normalize(g, lambda b: z1[:, g % 2, b * P:(b + 1) * P], w1_bank(g), rstd2, moments2).then_inc(done("norm2"), 1)

            def rest_(g):
                nb = blocks_of[g]
                three = dst_out[:, g % 2, 0:nb * PARTS * P].rearrange("p (b s f) -> p b s f", s=PARTS, f=P)
                r = rest[:, g % 2, 0:nb * P].rearrange("p (b f) -> p b f", b=nb)
                need(eng, "part0", g)
                need(eng, "part2", g - 2)
                eng.tensor_tensor(r, bank[5][:, 0:nb * P].rearrange("p (b f) -> p b f", b=nb), three[:, :, 0, :], ALU.subtract).then_inc(done("rest"), 1)

            def part2(g):
                nb = blocks_of[g]
                three = dst_out[:, g % 2, 0:nb * PARTS * P].rearrange("p (b s f) -> p b s f", s=PARTS, f=P)
                r = rest[:, g % 2, 0:nb * P].rearrange("p (b f) -> p b f", b=nb)
                need(eng, "part1", g)
                eng.tensor_tensor(three[:, :, 2, :], r, three[:, :, 1, :], ALU.subtract).then_inc(done("part2"), 1)

            run_stages(n_groups, [
                (4, norm1), (1, pre_), (2, soft_sum), (3, moments1_), (NORM2_AT, norm2), (5, moments2_),
                (DST_AT + 1, rest_), (DST_AT + 2, part2)])

            need(eng, "mean_mm", n_groups - 1)
            step(eng.memset(aggr, 0.0))

            def x1_offset(g):
                nb = blocks_of[g]
                need(eng, "x1_turn", g)
                x = x1_rows[:, g * GB:g * GB + nb, :]
                eng.tensor_tensor(x, x, wide["bt2"][:, :].unsqueeze(1).to_broadcast([P, nb, P]), ALU.add).then_inc(done("x1_offset"), 1)

            def hot3(c):
                if c % GROUP_EVERY == GROUP_EVERY - 1 and c // GROUP_EVERY < n_groups:
                    x1_offset(c // GROUP_EVERY)
                need(eng, "hot_turn", c - 3)
                make_onehot3(eng, onehot3[:, c % 3, :, :], lane_dst[:, c, :]).then_inc(done("hot3"), 1)

            def src_part(c):
                need(eng, "hidden", c)
                eng.wait_ge(gather_in[c % G_SLOTS], 16 * J * (c // G_SLOTS + 1))
                add_src_part(eng, hidden(c), gathered[:, c % G_SLOTS, :, :]).then_inc(done("hidden_sum"), 1)

            def logits(c):
                need(eng, "hidden_sum", c)
                need(eng, "weight", c - 4)
                edge_dots(eng, logit[:, c % 4, :], hidden(c)).then_inc(done("logit"), 1)

            def weigh_(c):
                need(eng, "weight", c)
                need(eng, "wsum", c - 3)
                weigh(eng, weighted[:, c % 3, :, :], lane_dst[:, c, :], weight[:, c % 4, :]).then_inc(done("weigh"), 1)

            def acc2(c):
                nonlocal regs
                if c % REGS == 0:
                    regs = load_starts(start_row, c, DVE)
                need(eng, "wsum", c)
                need(eng, "acc2", c - 1)
                add_window(eng, aggr, regs[c % REGS], W, window_out(c)).then_inc(done("acc2"), 1)

            run_stages(n_chunks, [(0, hot3), (4, weigh_), (3, src_part), (3, logits), (6, acc2)])
            for g in range(min(n_chunks // GROUP_EVERY, n_groups), n_groups):
                x1_offset(g)

            def far(item, c, start, first):
                far_item(item, c, start, first, W, far_dst[:, :])
                make_onehot3(eng, onehot3[:, 0, :, :], far_dst[:, :]).then_inc(done("far_hot3"), 1)
                eng.wait_ge(done("far_token"), item)
                eng.tensor_copy(far_src[:, :], lane_src[:, bass.ds(c * J, J)]).then_inc(done("far_src"), 1)
                eng.wait_ge(done("far_hidden"), item)
                eng.wait_ge(done("far_gather"), item * (16 * J))
                add_src_part(eng, hidden(0), gathered[:, 0, :, :])
                eng.drain()
                edge_dots(eng, logit[:, 0, :], hidden(0)).then_inc(done("far_logit"), 1)
                eng.wait_ge(done("far_weight"), item)
                weigh(eng, weighted[:, 0, :, :], far_dst[:, :], weight[:, 0, :]).then_inc(done("far_weigh"), 1)
                eng.wait_ge(done("far_wsum"), item)
                add_window(eng, aggr, start, W, window_out(0)).then_inc(done("far_acc2"), 1)
                eng.wait_ge(done("far_acc2"), item + 1)

            need(eng, "acc2", n_chunks - 1)
            eng.sem_inc(done("far_acc2"), 1)
            eng.sem_inc(done("far_token"), 1)
            further_windows(eng, 1, far)
            eng.sem_inc(done("acc2_all"), 1)

            def gate_logit(g):
                n = blocks_of[g] * P
                need(eng, "gate_mm", g)
                need(eng, "gate_h", g)
                need(eng, "mix_mul", g - 2)
                eng.tensor_tensor(pre[:, g % 2, 0:n], bank[g % 2][:, 0:n], gate_h[:, block_cols(g)], ALU.add).then_inc(done("gate_logit"), 1)

            def mix(g):
                cols = block_cols(g)
                need(eng, "mix_mul", g)
                eng.tensor_tensor(aggr[:, cols], y1[:, g % 2, 0:blocks_of[g] * P], h_cols[:, cols], ALU.add).then_inc(done("mix"), 1)

            def moments3(g):
                need(eng, "mix_rows", g)
                y = mix_rows[:, g * GB:g * GB + blocks_of[g], :].rearrange("p b f -> p (b f)")
                bn_moments(g, y, stats, moments_all[:, g * GB:g * GB + blocks_of[g], :], "moments3")

            run_stages(n_groups, [(0, gate_logit), (2, mix), (4, moments3)])
            need(eng, "rstd3", 0)
            eng.scalar_tensor_tensor(offset_all, moments_all[:, :, 0], -1.0, rstd_all, ALU.mult, ALU.mult).then_inc(done("offset3"), 1)

            def moments4(g):
                need(eng, "res2", g)
                row_moments(g, last_y[:, g % END_SLOTS, :], stats2, moments2, "out_rows", "moments4")

            def out_rows(g):
                need(eng, "rstd4", g)
                if g >= 2:
                    loaded(eng, f"out{g % 2}", out_dmas(g % 2, g))
                normalize(g, lambda b: y1[:, g % 2, b * P:(b + 1) * P], last_y[:, g % END_SLOTS, :], rstd2, moments2).then_inc(done("out_rows"), 1)

            run_stages(n_groups, [(2, out_rows), (1, moments4)])


N_SMALL = 18
NORM2_AT = 6
DST_AT = 10
DVE_BLOCKS = 2


def run_stages(n, stages):
    for t in range(n + max(d for d, _ in stages)):
        for d, f in stages:
            if 0 <= t - d < n:
                f(t - d)


def kernel(**inputs):
    import numpy as np
    import concourse.bacc as bacc
    from concourse.bass_utils import run_bass_kernel_spmd

    raw = {k: np.asarray(v) for k, v in inputs.items()}
    n_nodes, n_edges = raw["x"].shape[0], raw["src"].shape[0]

    def by_chunk(a):
        whole = (n_edges - 1) // CHUNK * CHUNK
        return np.concatenate([a[:whole], a[n_edges - CHUNK:]]).reshape(-1, CHUNK)

    def by_lane(a):
        return np.ascontiguousarray(by_chunk(a).reshape(-1, P, J).transpose(1, 0, 2))

    arrays = {
        "x": raw["x"], "x_t": np.ascontiguousarray(raw["x"].T), "edge_attr_128": raw["edge_attr_128"],
        "dst_by_chunk": by_chunk(raw["dst"]), "dst_by_lane": by_lane(raw["dst"]),
        "src_by_lane": by_lane(raw["src"]).reshape(P, -1),
        "L0_gnn_global_feats": raw["L0_gnn_global_feats"], "L0_W_t": np.ascontiguousarray(raw["L0_gnn_W"].T),
    }
    for name in ("W1", "b1", "g1", "bt1", "We1", "be1", "We2", "be2", "Wg", "bg", "g2", "bt2"):
        arrays["L1_gnn_" + name] = raw["L1_gnn_" + name]
    nc = bacc.Bacc("TRN2", target_bir_lowering=False, num_devices=1)
    io = {}
    for name, a in arrays.items():
        io[name] = nc.dram_tensor("in_" + name, a.shape, mybir.dt.from_np(a.dtype), kind="ExternalInput").ap()
    io["out"] = nc.dram_tensor("out_rows", (n_nodes, P), F32, kind="ExternalOutput").ap()
    gnn_pair(nc, n_nodes, n_edges, io)
    r = run_bass_kernel_spmd(nc, [{"in_" + k: np.ascontiguousarray(a) for k, a in arrays.items()}], core_ids=[0])
    return r.results[0]["out_rows"]
```
